# Optimizing a Trainium2 kernel written in Bass

```python
import numpy as np
import jax
import jax.numpy as jnp

def _softmax(x, axis=-1):
    return jax.nn.softmax(x, axis=axis)

def _gelu(x):
    return jax.nn.gelu(x, approximate=True)

def _silu(x):
    return jax.nn.silu(x)

def _sigmoid(x):
    return jax.nn.sigmoid(x)

def _layernorm(x, axis=-1, eps=1e-05):
    m = jnp.mean(x, axis=axis, keepdims=True)
    v = jnp.var(x, axis=axis, keepdims=True)
    return (x - m) / jnp.sqrt(v + eps)

def _scatter_add(tgt, idx, src, axis=0):
    return tgt.at[idx].add(src)

def _segment_sum(src, seg, n):
    return jax.ops.segment_sum(src, seg, n)
kernel_name = 'mk_adaln_ffn_d1_seqx_r4_6849df'

def setup_inputs(seed: int=0):
    np.random.seed(seed)
    _w = jnp.asarray

    def _rec_inputs():
        import jax
        import jax.numpy as jnp
        _rk = jax.random.key(seed)
        x = -7.109e-05 + 0.9999 * jax.random.normal(jax.random.fold_in(_rk, 1), (8, 256, 512), jnp.float32)
        _lenS = 256 - jax.random.randint(jax.random.fold_in(_rk, 7), (8,), 0, max(1, 256 // 4) + 1, jnp.int32)
        _lenS2 = 256 - jax.random.randint(jax.random.fold_in(_rk, 8), (8,), 0, max(1, 256 // 4) + 1, jnp.int32)
        itok_B_0_6 = jax.random.randint(jax.random.fold_in(_rk, 11), (8,), 0, 7, jnp.int32)
        return (x, itok_B_0_6)
    x, itok_B_0_6 = _rec_inputs()

    def _L0_cond_setup():
        import jax, jax.numpy as jnp
        import numpy as np
        B, T, D_IN, D_OUT = (16, 512, 512, 512)
        N_ADAPTERS, RANK = (8, 16)
        key = jax.random.key(seed)
        k_x, k_w, k_a, k_b, k_s, k_idx = jax.random.split(key, 6)
        x = jax.random.normal(k_x, (B, T, D_IN), dtype=jnp.float32)
        W = jax.random.normal(k_w, (D_OUT, D_IN), dtype=jnp.float32) * (1.0 / np.sqrt(D_IN))
        A = jax.random.normal(k_a, (N_ADAPTERS, RANK, D_IN), dtype=jnp.float32) * 0.02
        Bm = jax.random.normal(k_b, (N_ADAPTERS, D_OUT, RANK), dtype=jnp.float32) * 0.02
        scalings = jnp.ones((N_ADAPTERS,), dtype=jnp.float32)
        adapter_idx = jax.random.randint(k_idx, (B,), 0, N_ADAPTERS, dtype=jnp.int32)
        return {'x': x, 'W': W, 'A': A, 'Bm': Bm, 'scalings': scalings, 'adapter_idx': adapter_idx}
    _L0_cond_all = _L0_cond_setup()
    _L0_cond_in = {k: v for k, v in _L0_cond_all.items() if k in ('W', 'A', 'Bm', 'scalings')}
    del _L0_cond_all

    def _L0_ffn_setup():
        import jax, jax.numpy as jnp
        import numpy as np
        B, S, D = (4, 512, 512)
        E, K, M = (8, 2, 256)
        key = jax.random.key(seed)
        k0, k1, k2, k3, k4 = jax.random.split(key, 5)
        d_scale = D ** (-0.5)
        m_scale = M ** (-0.5)
        return {'x': jax.random.normal(k0, (B, S, D), jnp.float32), 'w_gate': jax.random.normal(k1, (D, E), jnp.float32) * d_scale, 'wi_0': jax.random.normal(k2, (E, D, M), jnp.float32) * d_scale, 'wi_1': jax.random.normal(k3, (E, D, M), jnp.float32) * d_scale, 'wo': jax.random.normal(k4, (E, M, D), jnp.float32) * m_scale}
    _L0_ffn_all = _L0_ffn_setup()
    _L0_ffn_in = {k: v for k, v in _L0_ffn_all.items() if k in ('w_gate', 'wi_0', 'wi_1', 'wo')}
    del _L0_ffn_all
    return {'x': x, 'itok_B_0_6': itok_B_0_6, 'L0_cond_W': _L0_cond_in['W'], 'L0_cond_A': _L0_cond_in['A'], 'L0_cond_Bm': _L0_cond_in['Bm'], 'L0_cond_scalings': _L0_cond_in['scalings'], 'L0_ffn_w_gate': _L0_ffn_in['w_gate'], 'L0_ffn_wi_0': _L0_ffn_in['wi_0'], 'L0_ffn_wi_1': _L0_ffn_in['wi_1'], 'L0_ffn_wo': _L0_ffn_in['wo']}

def reference(x, itok_B_0_6, L0_cond_W, L0_cond_A, L0_cond_Bm, L0_cond_scalings, L0_ffn_w_gate, L0_ffn_wi_0, L0_ffn_wi_1, L0_ffn_wo):
    import jax
    import jax.numpy as jnp

    def _L0_cond_ref(x, W, A, Bm, scalings, adapter_idx):
        import jax, jax.numpy as jnp
        import numpy as np
        B, T, D_IN, D_OUT = (16, 512, 512, 512)
        N_ADAPTERS, RANK = (8, 16)
        H = jnp.einsum('btd,od->bto', x, W)
        A_b = A[adapter_idx]
        B_b = Bm[adapter_idx]
        s_b = scalings[adapter_idx]
        xa = jnp.einsum('btd,brd->btr', x, A_b)
        delta = jnp.einsum('btr,bor->bto', xa, B_b)
        delta = jax.lax.stop_gradient(delta * s_b[:, None, None])
        return H + delta

    def _L0_ffn_ref(x, w_gate, wi_0, wi_1, wo):
        import jax, jax.numpy as jnp
        import numpy as np
        B, S, D = (4, 512, 512)
        E, K, M = (8, 2, 256)
        b, s, d = x.shape
        e = w_gate.shape[1]
        xf = x.reshape(-1, d)
        logits = jnp.dot(xf, w_gate)
        top_logits, top_idx = jax.lax.top_k(logits, K)
        weights = jax.nn.softmax(top_logits, axis=-1)
        flat_idx = top_idx.reshape(-1)
        sort_order = jnp.argsort(flat_idx)
        token_ids = sort_order // K
        sorted_x = jnp.take(xf, token_ids, axis=0)
        group_sizes = jnp.bincount(flat_idx, length=E).astype(jnp.int32)
        h0 = jax.lax.ragged_dot(sorted_x, wi_0, group_sizes)
        h1 = jax.lax.ragged_dot(sorted_x, wi_1, group_sizes)
        inter = jax.nn.silu(h0) * h1
        out_sorted = jax.lax.ragged_dot(inter, wo, group_sizes)
        unsort = jnp.argsort(sort_order)
        out = jnp.take(out_sorted, unsort, axis=0).reshape(-1, K, d)
        out = jnp.einsum('tkd,tk->td', out, weights)
        return out.reshape(b, s, d)
    x = x + _L0_ffn_ref(_L0_cond_ref(x, L0_cond_W, L0_cond_A, L0_cond_Bm, L0_cond_scalings, itok_B_0_6), L0_ffn_w_gate, L0_ffn_wi_0, L0_ffn_wi_1, L0_ffn_wo)
    return x

_drawn_inputs = setup_inputs


def setup_inputs(seed=0):
    import zlib

    import numpy as np

    out = dict(_drawn_inputs(seed))
    spreads = {'L0_cond_scalings': (1.0, 0.543)}
    factors = {}
    for name, (base, spread) in spreads.items():
        noise = np.random.default_rng([zlib.crc32(name.encode()), seed]).standard_normal(out[name].shape)
        drawn = base * np.exp(spread * noise) if base else spread * noise
        out[name] = jnp.asarray(drawn.astype(out[name].dtype))
    for name, factor in factors.items():
        out[name] = (out[name] * factor).astype(out[name].dtype)
    return out
```

```python
import numpy as np
import concourse.bass as bass
from concourse import mybir
from concourse.alu_op_type import AluOpType as ALU

F32, F32R = mybir.dt.float32, mybir.dt.float32r
BF16, I32, U32 = mybir.dt.bfloat16, mybir.dt.int32, mybir.dt.uint32
ACT = mybir.ActivationFunctionType
AX = mybir.AxisListType

P = 128
BATCHES, SEQ, D = 8, 256, 512
TOKENS = BATCHES * SEQ
HALVES = SEQ // P
KD = D // P
ADAPTERS, RANK = 8, 16
EXPERTS, TOP, M = 8, 2, 256
KM = M // P
GROUPS = 3
AROWS = GROUPS * 2 * RANK
PIECES = KD + KM
ALL_PIECES = EXPERTS * PIECES
PIECES_PER_BATCH = 5
LATE_PIECES = ALL_PIECES - PIECES_PER_BATCH * BATCHES
BLOCKS = TOKENS // P
TILES = TOP * TOKENS // P + EXPERTS - 1
ALL_BLOCKS = (EXPERTS - 1) * BLOCKS + TILES
SCRATCH = 4096

C_IDENT, C_UPPER, C_EXPERT, C_BASE, C_THR, C_TILE, C_TOK = 0, P, 2 * P, 2 * P + 8, 2 * P + 16, 2 * P + 32, 2 * P + 72
C_ALL = 2 * P + 76


def constants():
    c = np.zeros((P, C_ALL), np.float32)
    c[:, C_IDENT:C_IDENT + P] = np.eye(P)
    c[:, C_UPPER:C_UPPER + P] = np.triu(np.ones((P, P)), 1)
    c[:, C_EXPERT:C_EXPERT + EXPERTS] = np.arange(EXPERTS)
    c[:, C_BASE:C_BASE + EXPERTS] = np.arange(EXPERTS) * TOKENS
    c[:, C_THR:C_THR + BLOCKS] = np.arange(BLOCKS) * P
    c[:, C_TILE:C_TILE + 40] = np.arange(40)
    c[:, C_TOK:C_TOK + 4] = np.arange(P)[:, None] + np.array([0, 0, P, P]) - SEQ
    empty = np.zeros((ALL_BLOCKS * P, 2), np.int32)
    empty[:, 0] = TOKENS + np.arange(ALL_BLOCKS * P) % P
    return c, empty, np.zeros((P, D), np.float32)


def build(nc, xT, x, wT, aT, bT, scalings, adapter, w_gate, w_experts, consts, empty_list, zeros, out):
    y_rows = nc.dram_tensor("y_rows", (TOKENS + P, D), F32).ap()
    slots = nc.dram_tensor("slots", (ALL_BLOCKS * P, 2), I32).ap()

    top = [nc.sbuf_base + (-nc.sbuf_base) % 64]

    def size(shape, dt):
        n = {BF16: 2}.get(dt, 4)
        for s in shape[1:]:
            n *= s
        return n + (-n) % 32

    def put(name, shape, dt, at=None):
        if at is None:
            at = top[0]
            top[0] += size(shape, dt)
        return nc.alloc_sbuf_tensor_at(name, shape, dt, offset=at)

    hi_at = top[0]
    w_hi = put("w_hi", [P, ALL_PIECES, D], F32R)
    lo_at = top[0]
    w_lo = put("w_lo", [P, ALL_PIECES, D], F32R)
    piece = D * 4
    late = (ALL_PIECES - LATE_PIECES) * piece
    wt_hi = put("wt_hi", [P, KD, D], F32R, hi_at + late)
    wt_lo = put("wt_lo", [P, KD, D], F32R, hi_at + late + KD * piece)
    x_hi = put("x_hi", [P, 2, KD, SEQ], F32R, lo_at + late)
    x_lo = put("x_lo", [P, 2, KD, SEQ], F32R, lo_at + late + 2 * KD * SEQ * 4)
    wt_raw = put("wt_raw", [P, KD, D], F32, hi_at + 30 * piece)
    upper_raw = put("upper_raw", [P, P], F32, hi_at + 36 * piece)

    shared = top[0]
    yg = put("yg", [P, 2, D], F32)
    yt_hi = put("yt_hi", [P, 2, KD, P], F32R)
    yt_lo = put("yt_lo", [P, 2, KD, P], F32R)
    inter = put("inter", [P, M], F32)
    it_hi = put("it_hi", [P, 2, KM, P], F32R)
    it_lo = put("it_lo", [P, 2, KM, P], F32R)
    scaled = put("scaled", [P, 2, D], F32)
    end2 = top[0]
    top[0] = shared
    x_raw = put("x_raw", [P, KD, SEQ], F32)
    y_sb = put("y_sb", [P, 2, D], F32)
    yt_sb = put("yt_sb", [P, 2, KD, P], F32)
    a_raw = put("a_raw", [P, KD, RANK], F32)
    b_raw = put("b_raw", [AROWS, D], F32)
    a_hl = put("a_hl", [P, KD, GROUPS, 2, RANK], F32R)
    a_h0 = put("a_h0", [P, KD, GROUPS, 2, RANK], F32R)
    b_st = put("b_st", [AROWS, D], F32R)
    xa_st = put("xa_st", [AROWS, SEQ], F32R)
    cmp_n = put("cmp_n", [1, EXPERTS, BLOCKS], F32, shared)
    cmp_t = put("cmp_t", [1, TILES, EXPERTS - 1], F32, shared + 512)
    cmp_s = put("cmp_s", [1, TILES, EXPERTS - 1], F32, shared + 2048)
    best = put("best", [P, 2, 8], F32)
    best_at = put("best_at", [P, 2, 8], U32)
    best_f = put("best_f", [P, 2, TOP], F32)
    onehot = put("onehot", [P, 2, TOP, EXPERTS], F32)
    row_of = put("row_of", [P, 2, EXPERTS], F32)
    row_f = put("row_f", [P, 2 * TOP], F32)
    row_oh = put("row_oh", [P, 2, TOP, EXPERTS], F32)
    top[0] = max(top[0], end2)
    stage = put("stage", [P, 2, D], F32)
    ident = put("ident", [P, P], F32)
    upper = put("upper", [P, P], BF16)
    ones = put("ones", [P, P], BF16)
    wg = put("wg", [P, KD, EXPERTS], F32)
    smallc = put("smallc", [P, C_ALL - C_EXPERT], F32)
    expert_no = smallc[:, 0:8]
    base_row = smallc[:, C_BASE - C_EXPERT:C_BASE - C_EXPERT + 8]
    thresholds = smallc[0:1, C_THR - C_EXPERT:C_THR - C_EXPERT + BLOCKS]
    tile_no = smallc[0:1, C_TILE - C_EXPERT:C_TILE - C_EXPERT + TILES]
    token_no = smallc[:, C_TOK - C_EXPERT:C_TOK - C_EXPERT + 4]
    adapter_b = put("adapter_b", [AROWS, BATCHES], I32)
    adapter_f = put("adapter_f", [AROWS, BATCHES], F32)
    scal_b = put("scal_b", [AROWS, ADAPTERS], F32)
    scal_oh = put("scal_oh", [AROWS, BATCHES, ADAPTERS], F32, shared + 2 * KD * SEQ * 4)
    scal = put("scal", [AROWS, BATCHES], F32)
    chosen = put("chosen", [P, 2, EXPERTS], BF16)
    before = put("before", [P, 2, EXPERTS], BF16)
    gap = put("gap", [P, 2], F32)
    gap_exp = put("gap_exp", [P, 2], F32)
    gap_den = put("gap_den", [P, 2], F32)
    row_no = put("row_no", [P, 2 * TOP], I32)
    entry = put("entry", [P, 2 * TOP, 2], I32)
    n_tiles = put("n_tiles", [1, EXPERTS], F32)
    one8 = put("one8", [1, EXPERTS], F32)
    tile_end = put("tile_end", [1, EXPERTS], F32)
    expert_f = put("expert_f", [1, TILES], F32)
    start_f = put("start_f", [1, TILES], F32)
    block_f = put("block_f", [1, TILES], F32)
    expert_i = put("expert_i", [1, TILES], I32)
    block_i = put("block_i", [1, TILES], I32)
    g_list = put("g_list", [P, 2, 2], I32)
    s_list = put("s_list", [P, 2, 2], I32)
    assert top[0] <= nc.sbuf_usable_end

    bank = [nc.alloc_psum_tensor(f"bank{i}", [P, 512], F32) for i in range(8)]
    ps_y = [bank[0], bank[1]]
    ps_yt = bank[2]
    ps_log = bank[3][:, 0:2 * EXPERTS].rearrange("p (j e) -> p j e", j=2)
    ps_xa = bank[4][0:AROWS, 0:SEQ]
    ps_rank = bank[5][:, 0:2 * EXPERTS].rearrange("p (j e) -> p j e", j=2)
    ps_count = bank[6][:, 0:EXPERTS]
    ps_h = [bank[0], bank[1]]
    ps_it = bank[3]
    ps_o = [bank[4], bank[6]]

    S = nc.alloc_semaphore
    const_in, ident_in, wt_in, wg_in, idx_in, scal_in = S("const_in"), S("ident_in"), S("wt_in"), S("wg_in"), S("idx_in"), S("scal_in")
    upper_in = S("upper_in")
    x_in, a_in, b_in = S("x_in"), S("a_in"), S("b_in")
    piece_in = [S("piece_in0"), S("piece_in1")]
    y_stored = [S("y_stored0"), S("y_stored1")]
    out_is_x, out_pad, y_pad, slots_empty = S("out_is_x"), S("out_pad"), S("y_pad"), S("slots_empty")
    entry_out = [S(f"entry_out{i}") for i in range(2 * TOP)]
    g_list_in, s_list_in = [S("g_list_in0"), S("g_list_in1")], [S("s_list_in0"), S("s_list_in1")]
    yg_in = [S("yg_in0"), S("yg_in1")]
    added = S("added")
    wait_carried = S("wait_carried")
    setup_done, dve_chain, scal_done = S("setup_done"), S("dve_chain"), S("scal_done")
    wt_hi_done, wt_lo_done = S("wt_hi_done"), S("wt_lo_done")
    x_hi_done, x_lo_done = S("x_hi_done"), S("x_lo_done")
    a_hi_done, a_lo_done, b_hi_done, b_lo_done = S("a_hi_done"), S("a_lo_done"), S("b_hi_done"), S("b_lo_done")
    xa_done, xa_hi_done, xa_lo_done = S("xa_done"), S("xa_hi_done"), S("xa_lo_done")
    y_done, y_copied, yt_done, yt_copied = S("y_done"), S("y_copied"), S("yt_done"), S("yt_copied")
    logits_done, gap_done, gap_exp_done, chosen_done = S("logits_done"), S("gap_done"), S("gap_exp_done"), S("chosen_done")
    rank_done, entry_done, count_done, tables_done = S("rank_done"), S("entry_done"), S("count_done"), S("tables_done")
    p_hi_done, p_lo_dve, p_lo_pool = S("p_hi_done"), S("p_lo_dve"), S("p_lo_pool")
    t_yt, t_yt_hi, t_yt_lo = S("t_yt"), S("t_yt_hi"), S("t_yt_lo")
    t_up, t_silu, t_inter = S("t_up"), S("t_silu"), S("t_inter")
    t_it, t_it_hi, t_it_lo = S("t_it"), S("t_it_hi"), S("t_it_lo")
    t_down, t_scaled = S("t_down"), S("t_scaled")

    POOL_I, DVE_I = (0, 2, 4), (1, 3)

    def piece_free(i):
        before_b, i = (1, i - 2 + PIECES_PER_BATCH) if i < 2 else (0, i - 2)
        if i in POOL_I:
            return p_lo_pool, before_b, POOL_I.index(i) + 1, len(POOL_I)
        return p_lo_dve, before_b, DVE_I.index(i) + 1, len(DVE_I)

    def steady(engine, body):
        body(0, 0)
        body(1, 1)
        with engine.Fori(1, BATCHES // 2 - 1) as q:
            body(q * 2, 0)
            body(q * 2 + 1, 1)
        body(BATCHES - 2, 0)
        body(BATCHES - 1, 1)

    def known(b):
        return isinstance(b, int)

    def last(b):
        return known(b) and b == BATCHES - 1

    T0, T1 = 4, TILES - 1
    assert (T1 - T0) % 2 == 0

    def steps(engine, body, before_loop=range(-4, T0), after_loop=range(T1, TILES + 4)):
        for t in before_loop:
            body(t, t % 2, lambda i: 0 <= i < TILES)
        with engine.Fori(T0 // 2, (T1 + 1) // 2) as q:
            body(q * 2, 0, lambda i: True)
            body(q * 2 + 1, 1, lambda i: True)
        for t in after_loop:
            body(t, t % 2, lambda i: 0 <= i < TILES)

    def ok(i, live):
        return live(i) if isinstance(i, int) else True

    def uses(t, d, par):
        return (t - par) * 8 + 16 * ((par + d) // 2 + 1)

    def arrivals(b, par, i):
        return (b - par) * (PIECES_PER_BATCH * 8) + 16 * ((par * PIECES_PER_BATCH + i) // 2 + 1)

    block = nc.Block()
    with block:

        @block.sync
        def _(sp):
            sp.dma_start(x_raw[:], xT[0]).then_inc(x_in, 16)
            for k in range(KD):
                sp.dma_start(wt_raw[:, k], wT[:, k]).then_inc(wt_in, 16)
                sp.wait_ge(wt_in, 16 * (k + 1))
            sp.dma_start(adapter_b[:], adapter.partition_broadcast(AROWS)).then_inc(idx_in, 16)
            sp.wait_ge(idx_in, 16)

            def load_adapter(b):
                if known(b):
                    a = sp.value_load(adapter_b[0:1, b:b + 1], min_val=0, max_val=ADAPTERS - 1)
                else:
                    a = sp.value_load(adapter_b[0:1, bass.ds(b, 1)], min_val=0, max_val=ADAPTERS - 1)
                sp.dma_start(a_raw[:], aT[bass.ds(a, 1)].rearrange("a p k r -> (a p) k r")).then_inc(a_in, 16)
                sp.dma_start(b_raw[:], bT[bass.ds(a, 1)].rearrange("a p n -> (a p) n")).then_inc(b_in, 16)

            load_adapter(0)

            def load_piece(b, par, i):
                s = (par * PIECES_PER_BATCH + i) % 2
                g = b * PIECES_PER_BATCH + i
                src = w_experts[g] if known(b) else w_experts[bass.ds(sp.snap(g), 1)].rearrange("g p n -> (g p) n")
                lo_done, before_b, n, per = piece_free(i)
                if not (known(b) and b < before_b):
                    sp.wait_ge(lo_done, (b - before_b) * per + n)
                sp.dma_start(stage[:, s], src).then_inc(piece_in[s], 16)

            def store_y(b, j):
                r = b * SEQ + j * P
                dst = y_rows[r:r + P, :] if known(b) else y_rows[bass.ds(sp.snap(r), P), :]
                sp.wait_ge(y_copied, b * 2 + j + 1)
                sp.dma_start(dst, y_sb[:, j]).then_inc(y_stored[j], 16)

            def batch(b, par):
                if not (known(b) and b < 1):
                    store_y(b - 1, 1)
                if not last(b):
                    sp.wait_ge(x_lo_done, b + 1)
                    nxt = xT[b + 1] if known(b) else xT[bass.ds(b + 1, 1)].rearrange("b p k n -> (b p) k n")
                    sp.dma_start(x_raw[:], nxt).then_inc(x_in, 16)
                load_piece(b, par, 0)
                load_piece(b, par, 1)
                if not last(b):
                    sp.wait_ge(a_lo_done, b + 1)
                    sp.wait_ge(b_lo_done, b + 1)
                    load_adapter(b + 1)
                load_piece(b, par, 2)
                store_y(b, 0)
                load_piece(b, par, 3)
                load_piece(b, par, 4)

            steady(sp, batch)
            store_y(BATCHES - 1, 1)
            for g in range(ALL_PIECES - LATE_PIECES, ALL_PIECES):
                s = g % 2
                k = g - (ALL_PIECES - LATE_PIECES)
                if k == 0:
                    sp.wait_ge(p_lo_dve, len(DVE_I) * BATCHES)
                elif k == 1:
                    sp.wait_ge(p_lo_pool, len(POOL_I) * BATCHES)
                else:
                    sp.wait_ge(p_lo_dve, len(DVE_I) * BATCHES + k - 1)
                sp.dma_start(stage[:, s], w_experts[g]).then_inc(piece_in[s], 16)

            sp.wait_ge(tables_done, 1)
            for i in range(2 * TOP):
                sp.wait_ge(entry_out[i], 16 * BATCHES)
            sp.wait_ge(slots_empty, 16)

            def load_list(t, d, ring, sem, par):
                i = t + d
                if isinstance(t, int):
                    row = sp.value_load(block_i[0:1, i:i + 1], min_val=0, max_val=ALL_BLOCKS - 1)
                else:
                    row = sp.value_load(block_i[0:1, bass.ds(i, 1)], min_val=0, max_val=ALL_BLOCKS - 1)
                s = (par + d) % 2
                sp.dma_start(ring[:, s], slots[bass.ds(row * P, P), :]).then_inc(sem[s], 16)

            def step(t, par, live):
                if ok(t + 4, live) if isinstance(t, int) else True:
                    i = t + 4
                    if not (isinstance(i, int) and i < 2):
                        sp.wait_ge(yg_in[par], uses(t, 2, par))
                    load_list(t, 4, g_list, g_list_in, par)
                if ok(t - 1, live):
                    if not (isinstance(t, int) and t - 3 < 0):
                        sp.wait_ge(added, (t - 2) * 16)
                    load_list(t, -1, s_list, s_list_in, par)

            def step_in_loop(t, par, live):
                step(t, par, live)
            for t in range(-4, T0):
                step(t, t % 2, lambda i: 0 <= i < TILES)
            with sp.Fori(T0 // 2, (TILES - 5) // 2) as q:
                step(q * 2, 0, lambda i: True)
                step(q * 2 + 1, 1, lambda i: True)
            for t in range((TILES - 5) // 2 * 2, TILES + 4):
                step(t, t % 2, lambda i: 0 <= i < TILES)
            sp.wait_ge(added, 16 * TILES)

        @block.scalar
        def _(act):
            act.dma_start(smallc[:], consts[:, C_EXPERT:C_ALL]).then_inc(const_in, 16)
            act.dma_start(ident[:], consts[:, C_IDENT:C_IDENT + P]).then_inc(ident_in, 16)
            act.dma_start(upper_raw[:], consts[:, C_UPPER:C_UPPER + P]).then_inc(upper_in, 16)
            act.dma_start(wg[:], w_gate).then_inc(wg_in, 16)
            act.dma_start(scal_b[:], scalings.partition_broadcast(AROWS)).then_inc(scal_in, 16)
            act.dma_start(slots, empty_list).then_inc(slots_empty, 16)
            act.dma_start(out[TOKENS:TOKENS + P], zeros).then_inc(out_pad, 16)
            act.dma_start(y_rows[TOKENS:TOKENS + P], zeros).then_inc(y_pad, 16)

            def split_x(b, par):
                act.wait_ge(x_in, (b + 1) * 16)
                if not (known(b) and b < 2):
                    act.wait_ge(y_done, (b - 1) * 2)
                nc.scalar.copy(x_hi[:, par], x_raw[:]).then_inc(x_hi_done, 1)

            def split_a(b):
                act.wait_ge(a_in, (b + 1) * 16)
                if not (known(b) and b < 1):
                    act.wait_ge(xa_done, b)
                for k in range(KD):
                    src = a_raw[:, k].unsqueeze(1).to_broadcast([P, GROUPS, RANK])
                    nc.scalar.copy(a_hl[:, k, :, 0, :], src)
                    final = nc.scalar.copy(a_h0[:, k, :, 0, :], src)
                final.then_inc(a_hi_done, 1)

            def split_piece(b, par, i):
                s = (par * PIECES_PER_BATCH + i) % 2
                act.wait_ge(piece_in[s], arrivals(b, par, i))
                g = b * PIECES_PER_BATCH + i
                dst = w_hi[:, g] if known(b) else w_hi[:, bass.ds(g, 1)].rearrange("p a n -> p (a n)")
                nc.scalar.copy(dst, stage[:, s]).then_inc(p_hi_done, 1)

            def copy_y(b, j):
                act.wait_ge(y_done, b * 2 + j + 1)
                if not (known(b) and b < 1):
                    act.wait_ge(yt_done, (b - 1) * 2 + j + 1)
                    act.wait_ge(y_stored[j], b * 16)
                nc.scalar.copy(y_sb[:, j], ps_y[j][:]).then_inc(y_copied, 1)

            split_x(0, 0)
            for k in range(KD):
                act.wait_ge(wt_in, 16 * (k + 1))
                nc.scalar.copy(wt_hi[:, k], wt_raw[:, k]).then_inc(wt_hi_done, 1)
            act.wait_ge(setup_done, 1)
            split_a(0)
            act.wait_ge(scal_done, 1)

            def batch(b, par):
                if not (known(b) and b < 1):
                    copy_y(b - 1, 1)
                act.wait_ge(b_in, (b + 1) * 16)
                if not (known(b) and b < 1):
                    act.wait_ge(y_done, b * 2)
                nc.scalar.copy(b_st[:], b_raw[:]).then_inc(b_hi_done, 1)
                act.wait_ge(xa_done, b + 1)
                sc = scal[:, b:b + 1] if known(b) else scal[:, bass.ds(b, 1)]
                nc.scalar.activation(xa_st[:], ps_xa, ACT.Copy, scale=sc).then_inc(xa_hi_done, 1)
                if not (known(b) and b < 2):
                    exp_gap(b - 2)
                if not last(b):
                    split_x(b + 1, 1 - par)
                    split_a(b + 1)
                split_piece(b, par, 0)
                split_piece(b, par, 1)
                copy_y(b, 0)
                for i in range(2, PIECES_PER_BATCH):
                    split_piece(b, par, i)

            def exp_gap(b):
                act.wait_ge(gap_done, b + 1)
                nc.scalar.activation(gap_exp[:], gap[:], ACT.Exp).then_inc(gap_exp_done, 1)

            steady(act, batch)
            copy_y(BATCHES - 1, 1)
            exp_gap(BATCHES - 2)
            exp_gap(BATCHES - 1)
            act.wait_ge(y_done, 2 * BATCHES)
            for g in range(ALL_PIECES - LATE_PIECES, ALL_PIECES):
                act.wait_ge(piece_in[g % 2], 16 * (g // 2 + 1))
                nc.scalar.copy(w_hi[:, g], stage[:, g % 2]).then_inc(p_hi_done, 1)

            def step(t, par, live):
                if ok(t - 1, live):
                    act.wait_ge(t_up, t)
                    if not (isinstance(t, int) and t - 1 < 1):
                        act.wait_ge(t_it, t - 1)
                    nc.scalar.activation(inter[:], ps_h[(par + 1) % 2][:, 0:M], ACT.Silu).then_inc(t_silu, 1)
                if ok(t + 1, live):
                    act.wait_ge(t_yt, t + 2)
                    if not (isinstance(t, int) and t < 1):
                        act.wait_ge(t_up, t)
                    nc.scalar.copy(yt_hi[:, (par + 1) % 2], ps_yt[:].rearrange("p (k n) -> p k n", k=KD)).then_inc(t_yt_hi, 1)
                if ok(t - 3, live):
                    s = (par + 1) % 2
                    act.wait_ge(t_down, t - 2)
                    act.wait_ge(s_list_in[s], uses(t, -3, par))
                    if not (isinstance(t, int) and t - 3 < 2):
                        act.wait_ge(added, (t - 4) * 16)
                    nc.scalar.activation(scaled[:, s], ps_o[s][:], ACT.Copy,
                                         scale=s_list[:, s, 1:2].bitcast(F32)).then_inc(t_scaled, 1)
                if ok(t - 1, live):
                    act.wait_ge(t_it, t)
                    if not (isinstance(t, int) and t - 1 < 2):
                        act.wait_ge(t_down, t - 2)
                    nc.scalar.copy(it_hi[:, (par + 1) % 2], ps_it[:, 0:M].rearrange("p (k n) -> p k n", k=KM)).then_inc(t_it_hi, 1)

            steps(act, step)

        @block.vector
        def _(dve):
            chained = [0]

            def chain(ins):
                chained[0] += 1
                ins.then_inc(dve_chain, 1)
                dve.wait_ge(dve_chain, chained[0])

            V = nc.vector
            V.memset(a_h0[:].bitcast(F32), 0.0)
            V.memset(before[:], 0.0)
            V.memset(one8[:], 1.0)
            V.memset(ones[:], 1.0).then_inc(setup_done, 1)
            dve.wait_ge(idx_in, 16)
            dve.wait_ge(scal_in, 16)
            dve.wait_ge(const_in, 16)
            chain(V.tensor_copy(adapter_f[:], adapter_b[:]))
            chain(V.tensor_tensor(scal_oh[:], adapter_f[:].unsqueeze(2).to_broadcast([AROWS, BATCHES, ADAPTERS]),
                                  expert_no[0:AROWS].unsqueeze(1).to_broadcast([AROWS, BATCHES, ADAPTERS]), ALU.is_equal))
            chain(V.tensor_tensor(scal_oh[:], scal_oh[:], scal_b[:].unsqueeze(1).to_broadcast([AROWS, BATCHES, ADAPTERS]), ALU.mult))
            V.tensor_reduce(scal[:], scal_oh[:], AX.X, ALU.add).then_inc(scal_done, 1)

            def low(out, raw, high):
                return V.tensor_tensor(out, raw, high.bitcast(F32), ALU.subtract)

            def split_x(b, par):
                dve.wait_ge(x_hi_done, b + 1)
                low(x_lo[:, par], x_raw[:], x_hi[:, par]).then_inc(x_lo_done, 1)

            def split_a(b):
                dve.wait_ge(a_hi_done, b + 1)
                for k in range(KD):
                    final = low(a_hl[:, k, :, 1, :], a_raw[:, k].unsqueeze(1).to_broadcast([P, GROUPS, RANK]), a_hl[:, k, :, 0, :])
                final.then_inc(a_lo_done, 1)

            split_x(0, 0)
            for k in range(KD):
                dve.wait_ge(wt_hi_done, k + 1)
                low(wt_lo[:, k], wt_raw[:, k], wt_hi[:, k]).then_inc(wt_lo_done, 1)
            split_a(0)
            dve.wait_ge(upper_in, 16)
            V.tensor_copy(upper[:], upper_raw[:]).then_inc(setup_done, 1)

            def copy_yt(b, j):
                dve.wait_ge(yt_done, b * 2 + j + 1)
                if not (known(b) and b < 1):
                    dve.wait_ge(logits_done, (b - 1) * 2 + j + 1)
                V.tensor_copy(yt_sb[:, j], ps_yt[:].rearrange("p (k n) -> p k n", k=KD)).then_inc(yt_copied, 1)

            ROUTE = 12

            class link:
                def __init__(self, b):
                    self.b, self.n = b, 0

                def __call__(self, ins, wait=True):
                    self.n += 1
                    ins.then_inc(dve_chain, 1)
                    if wait:
                        dve.wait_ge(dve_chain, self.b * ROUTE + (SETUP + self.n))

                def skip(self):
                    dve.wait_ge(dve_chain, self.b * ROUTE + (SETUP + self.n))

            SETUP = chained[0]

            def choose(b, par, ln):
                dve.wait_ge(logits_done, (b + 1) * 2)
                V.tensor_scalar(token_no, token_no, float(SEQ), None, ALU.add)
                V.max(best[:, 0], ps_log[:, 0])
                ln(V.max(best[:, 1], ps_log[:, 1]))
                V.tensor_tensor(gap[:], best[:, :, 1], best[:, :, 0], ALU.subtract).then_inc(gap_done, 1)
                V.max_index(best_at[:, 0], best[:, 0], ps_log[:, 0])
                ln(V.max_index(best_at[:, 1], best[:, 1], ps_log[:, 1]))
                ln(V.tensor_copy(best_f[:], best_at[:, :, 0:TOP]))
                shape = [P, 2 * TOP, EXPERTS]
                ln(V.tensor_tensor(onehot[:].rearrange("p j k e -> p (j k) e"),
                                   best_f[:].rearrange("p j k -> p (j k)").unsqueeze(2).to_broadcast(shape),
                                   expert_no.unsqueeze(1).to_broadcast(shape), ALU.is_equal))
                if not (known(b) and b < 1):
                    dve.wait_ge(rank_done, b)
                ln(V.tensor_tensor(chosen[:], onehot[:, :, 0], onehot[:, :, 1], ALU.add))
                ln(V.tensor_tensor(before[:, 1 - par], before[:, par], chosen[:, 0], ALU.add))
                V.tensor_tensor(before[:, 1 - par], before[:, 1 - par], chosen[:, 1], ALU.add).then_inc(chosen_done, 1)

            def weigh(b, ln):
                dve.wait_ge(gap_exp_done, b + 1)
                if not (known(b) and b < 1):
                    for i in range(2 * TOP):
                        dve.wait_ge(entry_out[i], b * 16)
                e = entry[:].bitcast(F32).rearrange("p (j k) c -> p j k c", j=2)
                ln(V.tensor_scalar(gap_den[:], gap_exp[:], 1.0, None, ALU.add))
                ln(V.reciprocal(e[:, :, 0, 1], gap_den[:]))
                V.tensor_tensor(e[:, :, 1, 1], gap_exp[:], e[:, :, 0, 1], ALU.mult)
                ln(V.tensor_copy(entry[:, :, 0], token_no))

            def place(b, ln):
                dve.wait_ge(rank_done, b + 1)
                ln(V.tensor_tensor(row_of[:], ps_rank, base_row.unsqueeze(1).to_broadcast([P, 2, EXPERTS]), ALU.add))
                for k in range(TOP):
                    final = V.tensor_tensor(row_oh[:, :, k], onehot[:, :, k], row_of[:], ALU.mult)
                ln(final)
                ln(V.tensor_reduce(row_f[:], row_oh[:].rearrange("p j k e -> p (j k) e"), AX.X, ALU.add))
                assert ln.n == ROUTE
                V.tensor_copy(row_no[:], row_f[:]).then_inc(entry_done, 1)

            def split_piece(b, par, i):
                s = (par * PIECES_PER_BATCH + i) % 2
                dve.wait_ge(p_hi_done, b * PIECES_PER_BATCH + i + 1)
                g = b * PIECES_PER_BATCH + i
                if known(b):
                    dst, hi = w_lo[:, g], w_hi[:, g]
                else:
                    dst, hi = [w[:, bass.ds(g, 1)].rearrange("p a n -> p (a n)") for w in (w_lo, w_hi)]
                low(dst, stage[:, s], hi).then_inc(p_lo_dve, 1)

            def batch(b, par):
                if not (known(b) and b < 1):
                    copy_yt(b - 1, 0)
                third = 2 * RANK
                dve.wait_ge(b_hi_done, b + 1)
                low(b_st[2 * third:], b_raw[2 * third:], b_st[2 * third:]).then_inc(b_lo_done, 1)
                dve.wait_ge(xa_hi_done, b + 1)
                sc = scal[third:2 * third, b:b + 1] if known(b) else scal[third:2 * third, bass.ds(b, 1)]
                V.scalar_tensor_tensor(xa_st[third:2 * third], ps_xa[third:2 * third], sc, xa_st[third:2 * third].bitcast(F32),
                                       ALU.mult, ALU.subtract).then_inc(xa_lo_done, 1)
                two = not (known(b) and b < 2)
                ln = link(b - 2) if two else None
                if two:
                    choose(b - 2, par, ln)
                if not last(b):
                    split_x(b + 1, 1 - par)
                    split_a(b + 1)
                if two:
                    weigh(b - 2, ln)
                split_piece(b, par, DVE_I[0])
                if not (known(b) and b < 1):
                    copy_yt(b - 1, 1)
                if two:
                    place(b - 2, ln)
                split_piece(b, par, DVE_I[1])

            steady(dve, batch)
            for b in (BATCHES - 2, BATCHES - 1):
                ln = link(b)
                if b == BATCHES - 2:
                    copy_yt(BATCHES - 1, 0)
                choose(b, b % 2, ln)
                if b == BATCHES - 2:
                    copy_yt(BATCHES - 1, 1)
                weigh(b, ln)
                place(b, ln)
            chained[0] = SETUP + ROUTE * BATCHES
            dve.wait_ge(count_done, 1)
            shape = [1, EXPERTS, BLOCKS]
            chain(V.tensor_tensor(cmp_n[:], ps_count[0:1].unsqueeze(2).to_broadcast(shape),
                                  thresholds.unsqueeze(1).to_broadcast(shape), ALU.is_gt))
            chain(V.tensor_reduce(n_tiles[:], cmp_n[:], AX.X, ALU.add))
            chain(V.tensor_tensor_scan(tile_end[:], one8[:], n_tiles[:], 0.0, ALU.mult, ALU.add))
            shape = [1, TILES, EXPERTS - 1]
            chain(V.tensor_tensor(cmp_t[:], tile_no.unsqueeze(2).to_broadcast(shape),
                                  tile_end[:, 0:EXPERTS - 1].unsqueeze(1).to_broadcast(shape), ALU.is_ge))
            V.tensor_tensor(cmp_s[:], cmp_t[:], n_tiles[:, 0:EXPERTS - 1].unsqueeze(1).to_broadcast(shape), ALU.mult)
            chain(V.tensor_reduce(expert_f[:], cmp_t[:], AX.X, ALU.add))
            chain(V.tensor_reduce(start_f[:], cmp_s[:], AX.X, ALU.add))
            V.tensor_copy(expert_i[:], expert_f[:])
            chain(V.scalar_tensor_tensor(block_f[:], expert_f[:], float(BLOCKS), tile_no, ALU.mult, ALU.add))
            V.tensor_tensor(block_i[:], block_f[:], start_f[:], ALU.subtract).then_inc(tables_done, 1)
            for g in range(ALL_PIECES - LATE_PIECES, ALL_PIECES):
                dve.wait_ge(p_hi_done, g + 1)
                low(w_lo[:, g], stage[:, g % 2], w_hi[:, g]).then_inc(p_lo_dve, 1)

            def step(t, par, live):
                if ok(t - 1, live):
                    dve.wait_ge(t_silu, t)
                    V.tensor_tensor(inter[:], inter[:], ps_h[(par + 1) % 2][:, M:2 * M], ALU.mult).then_inc(t_inter, 1)
                if ok(t + 1, live):
                    dve.wait_ge(t_yt_hi, t + 2)
                    s = (par + 1) % 2
                    low(yt_lo[:, s], ps_yt[:].rearrange("p (k n) -> p k n", k=KD), yt_hi[:, s]).then_inc(t_yt_lo, 1)
                if ok(t - 1, live):
                    dve.wait_ge(t_it_hi, t)
                    s = (par + 1) % 2
                    low(it_lo[:, s], ps_it[:, 0:M].rearrange("p (k n) -> p k n", k=KM), it_hi[:, s]).then_inc(t_it_lo, 1)

            steps(dve, step)

        @block.gpsimd
        def _(pool):
            pool.dma_start(out[0:TOKENS], x).then_inc(out_is_x, 16)

            def carry_wait():
                pool.sem_inc(wait_carried, 1)

            pool.wait_ge(slots_empty, 16)

            def split_piece(b, par, i):
                s = (par * PIECES_PER_BATCH + i) % 2
                pool.wait_ge(p_hi_done, b * PIECES_PER_BATCH + i + 1)
                g = b * PIECES_PER_BATCH + i
                if known(b):
                    dst, hi = w_lo[:, g], w_hi[:, g]
                else:
                    dst, hi = [w[:, bass.ds(g, 1)].rearrange("p a n -> p (a n)") for w in (w_lo, w_hi)]
                nc.gpsimd.tensor_tensor(dst, stage[:, s], hi.bitcast(F32), ALU.subtract).then_inc(p_lo_pool, 1)

            def list_entries(b):
                pool.wait_ge(entry_done, b + 1)
                carry_wait()
                for i in range(2 * TOP):
                    pool.indirect_dma_start(slots, bass.IndirectOffsetOnAxis(row_no[:, i:i + 1], 0), entry[:, i], None).then_inc(entry_out[i], 16)

            def batch(b, par):
                for i in POOL_I[:2]:
                    split_piece(b, par, i)
                if not (known(b) and b < 2):
                    list_entries(b - 2)
                for i in POOL_I[2:]:
                    split_piece(b, par, i)

            steady(pool, batch)
            list_entries(BATCHES - 2)
            list_entries(BATCHES - 1)
            for j in range(2):
                pool.wait_ge(y_stored[j], 16 * BATCHES)
            pool.wait_ge(y_pad, 16)
            pool.wait_ge(out_pad, 16)
            pool.wait_ge(out_is_x, 16)

            def step(t, par, live):
                if ok(t + 2, live):
                    pool.wait_ge(g_list_in[par], uses(t, 2, par))
                    if not (isinstance(t, int) and t < 0):
                        pool.wait_ge(t_yt, t + 1)
                    carry_wait()
                    pool.indirect_dma_start(yg[:, par], None, y_rows, bass.IndirectOffsetOnAxis(g_list[:, par, 0:1], 0)).then_inc(yg_in[par], 16)
                if ok(t - 3, live):
                    s = (par + 1) % 2
                    pool.wait_ge(t_scaled, t - 2)
                    if not (isinstance(t, int) and t - 3 < 1):
                        pool.wait_ge(added, (t - 3) * 16)
                    carry_wait()
                    pool.indirect_dma_start(out, bass.IndirectOffsetOnAxis(s_list[:, s, 0:1], 0), scaled[:, s], None,
                                            compute_op=ALU.add).then_inc(added, 16)

            for t in range(-4, T0):
                step(t, t % 2, lambda i: 0 <= i < TILES)
            with pool.Fori(T0 // 2, (TILES - 3) // 2) as q:
                step(q * 2, 0, lambda i: True)
                step(q * 2 + 1, 1, lambda i: True)
            for t in range((TILES - 3) // 2 * 2, TILES + 4):
                step(t, t % 2, lambda i: 0 <= i < TILES)

        @block.tensor
        def _(pe):
            mm = nc.tensor.matmul

            def adapter_in(b, par):
                pe.wait_ge(x_lo_done, b + 1)
                pe.wait_ge(a_lo_done, b + 1)
                if not (known(b) and b < 1):
                    pe.wait_ge(xa_lo_done, b)
                for k in range(KD):
                    mm(ps_xa, a_hl[:, k].rearrange("p g c r -> p (g c r)"), x_hi[:, par, k], start=(k == 0), stop=False)
                    final = mm(ps_xa, a_h0[:, k].rearrange("p g c r -> p (g c r)"), x_lo[:, par, k], start=False, stop=(k == KD - 1))
                final.then_inc(xa_done, 1)

            def base(b, par, j):
                if not (known(b) and b < 1):
                    pe.wait_ge(y_copied, (b - 1) * 2 + j + 1)
                cols = slice(j * P, (j + 1) * P)
                for k in range(KD):
                    if known(b) and b == 0 and j == 0:
                        pe.wait_ge(wt_lo_done, k + 1)
                    mm(ps_y[j][:], x_hi[:, par, k, cols], wt_hi[:, k], start=(k == 0), stop=False)
                    mm(ps_y[j][:], x_hi[:, par, k, cols], wt_lo[:, k], start=False, stop=False)
                    mm(ps_y[j][:], x_lo[:, par, k, cols], wt_hi[:, k], start=False, stop=False)

            def delta(b, j):
                if j == 0:
                    pe.wait_ge(xa_lo_done, b + 1)
                    pe.wait_ge(b_lo_done, b + 1)
                mm(ps_y[j][:], xa_st[:, j * P:(j + 1) * P], b_st[:], start=False, stop=True).then_inc(y_done, 1)

            def turn_y(b, j):
                pe.wait_ge(y_copied, b * 2 + j + 1)
                if j == 1:
                    pe.wait_ge(yt_copied, b * 2 + 1)
                elif not (known(b) and b < 1):
                    pe.wait_ge(yt_copied, b * 2)
                for k in range(KD):
                    final = nc.tensor.transpose(ps_yt[:, k * P:(k + 1) * P], y_sb[:, j, k * P:(k + 1) * P], ident[:])
                final.then_inc(yt_done, 1)

            def logits(b, j):
                pe.wait_ge(yt_copied, b * 2 + j + 1)
                if j == 0 and not (known(b) and b < 1):
                    pe.wait_ge(chosen_done, b)
                for k in range(KD):
                    final = mm(ps_log[:, j], yt_sb[:, j, k], wg[:, k], start=(k == 0), stop=(k == KD - 1))
                final.then_inc(logits_done, 1)

            def rank(b, par):
                pe.wait_ge(chosen_done, b + 1)
                if not (known(b) and b < 1):
                    pe.wait_ge(entry_done, b)
                mm(ps_rank[:, 0], upper[:], chosen[:, 0], start=True, stop=False)
                mm(ps_rank[:, 0], ones[:], before[:, par], start=False, stop=True)
                mm(ps_rank[:, 1], upper[:], chosen[:, 1], start=True, stop=False)
                mm(ps_rank[:, 1], ones[:], chosen[:, 0], start=False, stop=False)
                mm(ps_rank[:, 1], ones[:], before[:, par], start=False, stop=True).then_inc(rank_done, 1)

            pe.wait_ge(ident_in, 16)
            pe.wait_ge(wg_in, 16)
            pe.wait_ge(setup_done, 2)

            def batch(b, par):
                one, two = not (known(b) and b < 1), not (known(b) and b < 2)
                adapter_in(b, par)
                base(b, par, 0)
                if one:
                    logits(b - 1, 0)
                if two:
                    rank(b - 2, par)
                if one:
                    turn_y(b - 1, 1)
                delta(b, 0)
                base(b, par, 1)
                if one:
                    logits(b - 1, 1)
                turn_y(b, 0)
                delta(b, 1)

            steady(pe, batch)
            b = BATCHES - 1
            logits(b, 0)
            rank(b - 1, 0)
            turn_y(b, 1)
            logits(b, 1)
            rank(b, 1)
            mm(ps_count, ones[:], before[:, 0], start=True, stop=True).then_inc(count_done, 1)

            pe.wait_ge(p_lo_pool, len(POOL_I) * BATCHES)
            pe.wait_ge(p_lo_dve, len(DVE_I) * BATCHES + LATE_PIECES)
            pe.wait_ge(tables_done, 1)
            pe.wait_ge(yt_copied, 2 * BATCHES)
            pe.wait_ge(entry_done, BATCHES)

            def step(t, par, live):
                nxt = (par + 1) % 2
                if ok(t + 1, live):
                    pe.wait_ge(yg_in[nxt], uses(t, 1, par))
                    if not (isinstance(t, int) and t + 1 < 1):
                        pe.wait_ge(t_yt_lo, t + 1)
                    for k in range(KD):
                        final = nc.tensor.transpose(ps_yt[:, k * P:(k + 1) * P], yg[:, nxt, k * P:(k + 1) * P], ident[:])
                    final.then_inc(t_yt, 1)
                if ok(t, live):
                    i = slice(t, t + 1) if isinstance(t, int) else bass.ds(t, 1)
                    e = pe.value_load(expert_i[0:1, i], min_val=0, max_val=EXPERTS - 1)
                    pe.wait_ge(t_yt_lo, t + 1)
                    if not (isinstance(t, int) and t < 2):
                        pe.wait_ge(t_inter, t - 1)
                    h = ps_h[par][:]
                    for k in range(KD):
                        hi = w_hi[:, bass.ds(e * PIECES + k, 1)].rearrange("p a n -> p (a n)")
                        lo = w_lo[:, bass.ds(e * PIECES + k, 1)].rearrange("p a n -> p (a n)")
                        mm(h, yt_hi[:, par, k], hi, start=(k == 0), stop=False)
                        mm(h, yt_lo[:, par, k], hi, start=False, stop=False)
                        final = mm(h, yt_hi[:, par, k], lo, start=False, stop=(k == KD - 1))
                    final.then_inc(t_up, 1)
                if ok(t - 1, live):
                    pe.wait_ge(t_inter, t)
                    if not (isinstance(t, int) and t - 1 < 1):
                        pe.wait_ge(t_it_lo, t - 1)
                    for k in range(KM):
                        final = nc.tensor.transpose(ps_it[:, k * P:(k + 1) * P], inter[:, k * P:(k + 1) * P], ident[:])
                    final.then_inc(t_it, 1)
                if ok(t - 2, live):
                    i = slice(t - 2, t - 1) if isinstance(t, int) else bass.ds(t - 2, 1)
                    e = pe.value_load(expert_i[0:1, i], min_val=0, max_val=EXPERTS - 1)
                    pe.wait_ge(t_it_lo, t - 1)
                    if not (isinstance(t, int) and t - 2 < 2):
                        pe.wait_ge(t_scaled, t - 3)
                    o = ps_o[par][:]
                    for k in range(KM):
                        hi = w_hi[:, bass.ds(e * PIECES + KD + k, 1)].rearrange("p a n -> p (a n)")
                        lo = w_lo[:, bass.ds(e * PIECES + KD + k, 1)].rearrange("p a n -> p (a n)")
                        mm(o, it_hi[:, par, k], hi, start=(k == 0), stop=False)
                        mm(o, it_lo[:, par, k], hi, start=False, stop=False)
                        final = mm(o, it_hi[:, par, k], lo, start=False, stop=(k == KM - 1))
                    final.then_inc(t_down, 1)

            steps(pe, step)


def kernel(**inputs):
    import concourse.bacc as bacc
    from concourse.bass_utils import run_bass_kernel_spmd as run

    n = {k: np.asarray(v) for k, v in inputs.items()}
    x = np.ascontiguousarray(n["x"].reshape(TOKENS, D))
    consts, empty_list, zeros = constants()
    wi = np.concatenate([n["L0_ffn_wi_0"], n["L0_ffn_wi_1"]], axis=2).reshape(EXPERTS, KD, P, 2 * M)
    wo = n["L0_ffn_wo"].reshape(EXPERTS, KM, P, D)
    a = n["L0_cond_A"].reshape(ADAPTERS, RANK, KD, P).transpose(0, 3, 2, 1)
    b = np.tile(n["L0_cond_Bm"].transpose(0, 2, 1), (1, 2 * GROUPS, 1))
    arrays = {
        "xT": x.reshape(BATCHES, SEQ, KD, P).transpose(0, 3, 2, 1),
        "x": x,
        "wT": n["L0_cond_W"].T.reshape(KD, P, D).transpose(1, 0, 2),
        "aT": a,
        "bT": b,
        "scalings": n["L0_cond_scalings"],
        "adapter": n["itok_B_0_6"],
        "w_gate": n["L0_ffn_w_gate"].reshape(KD, P, EXPERTS).transpose(1, 0, 2),
        "w_experts": np.concatenate([wi, wo], axis=1).reshape(ALL_PIECES, P, D),
        "consts": consts,
        "empty_list": empty_list,
        "zeros": zeros,
    }
    nc = bacc.Bacc("TRN2", target_bir_lowering=False, num_devices=1, dynamic_dma_scratch_size=SCRATCH)
    given, aps = {}, {}
    for name, v in arrays.items():
        v = np.ascontiguousarray(v)
        given[f"in_{name}"] = v
        aps[name] = nc.dram_tensor(f"in_{name}", v.shape, mybir.dt.from_np(v.dtype), kind="ExternalInput").ap()
    out = nc.dram_tensor("out_0", (TOKENS + P, D), F32, kind="ExternalOutput").ap()
    build(nc, out=out, **aps)
    r = run(nc, [given], core_ids=[0])
    return r.results[0]["out_0"][:TOKENS].reshape(BATCHES, SEQ, D)
```

```python
import numpy as np
import concourse.bass as bass
from concourse import mybir
from concourse.alu_op_type import AluOpType as ALU

F32, F32R = mybir.dt.float32, mybir.dt.float32r
BF16, I32, U32 = mybir.dt.bfloat16, mybir.dt.int32, mybir.dt.uint32
ACT = mybir.ActivationFunctionType
AX = mybir.AxisListType

P = 128
BATCHES, SEQ, D = 8, 256, 512
TOKENS = BATCHES * SEQ
HALVES = SEQ // P
KD = D // P
ADAPTERS, RANK = 8, 16
EXPERTS, TOP, M = 8, 2, 256
KM = M // P
GROUPS = 3
AROWS = GROUPS * 2 * RANK
PIECES = KD + KM
PAIRS = PIECES // 2
BLOCKS = TOKENS // P
TILES = TOP * TOKENS // P + EXPERTS - 1
ALL_BLOCKS = (EXPERTS - 1) * BLOCKS + TILES
SCRATCH = 4096

C_IDENT, C_UPPER, C_EXPERT, C_BASE, C_THR, C_TILE, C_TOK = 0, P, 2 * P, 2 * P + 8, 2 * P + 16, 2 * P + 32, 2 * P + 72
C_ALL = 2 * P + 76


def constants():
    c = np.zeros((P, C_ALL), np.float32)
    c[:, C_IDENT:C_IDENT + P] = np.eye(P)
    c[:, C_UPPER:C_UPPER + P] = np.triu(np.ones((P, P)), 1)
    c[:, C_EXPERT:C_EXPERT + EXPERTS] = np.arange(EXPERTS)
    c[:, C_BASE:C_BASE + EXPERTS] = np.arange(EXPERTS) * TOKENS
    c[:, C_THR:C_THR + BLOCKS] = np.arange(BLOCKS) * P
    c[:, C_TILE:C_TILE + 40] = np.arange(40)
    c[:, C_TOK:C_TOK + 4] = np.arange(P)[:, None] + np.array([0, 0, P, P]) - SEQ
    empty = np.zeros((ALL_BLOCKS * P, 2), np.int32)
    empty[:, 0] = TOKENS + np.arange(ALL_BLOCKS * P) % P
    return c, empty, np.zeros((P, D), np.float32)


def build(nc, xT, x, wT, aT, bT, scalings, adapter, w_gate, wi, wo, consts, empty_list, zeros, out):
    y_rows = nc.dram_tensor("y_rows", (TOKENS + P, D), F32).ap()
    slots = nc.dram_tensor("slots", (ALL_BLOCKS * P, 2), I32).ap()

    top = [nc.sbuf_base + (-nc.sbuf_base) % 64]

    def size(shape, dt):
        n = {BF16: 2}.get(dt, 4)
        for s in shape[1:]:
            n *= s
        return n + (-n) % 32

    def put(name, shape, dt, at=None):
        if at is None:
            at = top[0]
            top[0] += size(shape, dt)
        return nc.alloc_sbuf_tensor_at(name, shape, dt, offset=at)

    wi_hi = put("wi_hi", [P, EXPERTS, KD, D], F32R)
    wo_hi = put("wo_hi", [P, EXPERTS, KM, D], F32R)
    wi_lo_at = top[0]
    wi_lo = put("wi_lo", [P, EXPERTS, KD, D], F32R)
    wo_lo_at = top[0]
    wo_lo = put("wo_lo", [P, EXPERTS, KM, D], F32R)
    w_hi, w_lo = (wi_hi, wo_hi), (wi_lo, wo_lo)
    w_raw = (put("wi_raw", [P, EXPERTS, KD, D], F32, wi_lo_at), put("wo_raw", [P, EXPERTS, KM, D], F32, wo_lo_at))

    wi_expert, wo_expert = KD * D * 4, KM * D * 4
    wi_hi_at, wo_hi_at = wi_lo_at - EXPERTS * (wi_expert + wo_expert), wi_lo_at - EXPERTS * wo_expert
    wt_hi = put("wt_hi", [P, KD, D], F32R, wi_hi_at + (EXPERTS - 1) * wi_expert)
    y_sb = put("y_sb", [P, 2, D], F32, wo_hi_at + (EXPERTS - 1) * wo_expert)
    wt_lo = put("wt_lo", [P, KD, D], F32R, wi_lo_at + (EXPERTS - 1) * wi_expert)
    wt_raw = put("wt_raw", [P, KD, D], F32, wi_lo_at + (EXPERTS - 1) * wi_expert)
    yt_sb = put("yt_sb", [P, 2, KD, P], F32, wo_lo_at + (EXPERTS - 1) * wo_expert)

    sixth = wi_hi_at + (EXPERTS - 2) * wi_expert
    upper_raw = put("upper_raw", [P, P], F32, sixth)
    scal_oh = put("scal_oh", [AROWS, BATCHES, ADAPTERS], F32, sixth + P * 4)

    shared = top[0]
    yg = put("yg", [P, 2, D], F32)
    yt_hi = put("yt_hi", [P, 2, KD, P], F32R)
    yt_lo = put("yt_lo", [P, 2, KD, P], F32R)
    inter = put("inter", [P, M], F32)
    it_hi = put("it_hi", [P, 2, KM, P], F32R)
    it_lo = put("it_lo", [P, 2, KM, P], F32R)
    scaled = put("scaled", [P, 2, D], F32)
    end2 = top[0]
    top[0] = shared
    x_hi = put("x_hi", [P, 2, KD, SEQ], F32R)
    x_lo = put("x_lo", [P, 2, KD, SEQ], F32R)
    x_raw = put("x_raw", [P, 2, KD, SEQ], F32, top[0] - 2 * KD * SEQ * 4)
    a_raw = put("a_raw", [P, KD * GROUPS, RANK], F32)
    b_raw = put("b_raw", [AROWS, D], F32)
    a_hl = put("a_hl", [P, KD * GROUPS, 2, RANK], F32R)
    a_h0 = put("a_h0", [P, KD * GROUPS, 2, RANK], F32R)
    b_st = put("b_st", [AROWS, D], F32R)
    xa_st = put("xa_st", [AROWS, SEQ], F32R)
    cmp_n = put("cmp_n", [1, EXPERTS, BLOCKS], F32, shared)
    cmp_t = put("cmp_t", [1, TILES, EXPERTS - 1], F32, shared + 512)
    cmp_s = put("cmp_s", [1, TILES, EXPERTS - 1], F32, shared + 2048)
    expert_f = put("expert_f", [1, TILES], F32, shared + 3200)
    start_f = put("start_f", [1, TILES], F32, shared + 3392)
    block_f = put("block_f", [1, TILES], F32, shared + 3584)
    best = put("best", [P, 2, 8], F32)
    best_at = put("best_at", [P, 2, 8], U32)
    best_f = put("best_f", [P, 2, TOP], F32)
    onehot = put("onehot", [P, 2, TOP, EXPERTS], F32)
    row_of = put("row_of", [P, 2, EXPERTS], F32)
    row_f = put("row_f", [P, 2 * TOP], F32)
    row_oh = put("row_oh", [P, 2, TOP, EXPERTS], F32)
    top[0] = max(top[0], end2)
    ident = put("ident", [P, P], F32)
    upper = put("upper", [P, P], BF16)
    ones = put("ones", [P, P], BF16)
    wg = put("wg", [P, KD, EXPERTS], F32)
    smallc = put("smallc", [P, C_ALL - C_EXPERT], F32)
    expert_no = smallc[:, 0:8]
    base_row = smallc[:, C_BASE - C_EXPERT:C_BASE - C_EXPERT + 8]
    thresholds = smallc[0:1, C_THR - C_EXPERT:C_THR - C_EXPERT + BLOCKS]
    tile_no = smallc[0:1, C_TILE - C_EXPERT:C_TILE - C_EXPERT + TILES]
    token_no = smallc[:, C_TOK - C_EXPERT:C_TOK - C_EXPERT + 4]
    adapter_b = put("adapter_b", [AROWS, BATCHES], I32)
    adapter_f = put("adapter_f", [AROWS, BATCHES], F32)
    scal_b = put("scal_b", [AROWS, ADAPTERS], F32)
    scal = put("scal", [AROWS, BATCHES], F32)
    chosen = put("chosen", [P, 2, EXPERTS], BF16)
    before = put("before", [P, 2, EXPERTS], BF16)
    gap = put("gap", [P, 2], F32)
    gap_exp = put("gap_exp", [P, 2], F32)
    gap_den = put("gap_den", [P, 2], F32)
    row_no = put("row_no", [P, 2 * TOP], I32)
    entry = put("entry", [P, 2 * TOP, 2], I32)
    n_tiles = put("n_tiles", [1, EXPERTS], F32)
    one8 = put("one8", [1, EXPERTS], F32)
    tile_end = put("tile_end", [1, EXPERTS], F32)
    expert_i = put("expert_i", [1, TILES], I32)
    block_i = put("block_i", [1, TILES], I32)
    g_list = put("g_list", [P, 2, 2], I32)
    s_list = put("s_list", [P, 2, 2], I32)
    assert top[0] <= nc.sbuf_usable_end

    bank = [nc.alloc_psum_tensor(f"bank{i}", [P, 512], F32) for i in range(8)]
    ps_y = [bank[0], bank[1]]
    ps_yt = bank[2]
    ps_log = bank[3][:, 0:2 * EXPERTS].rearrange("p (j e) -> p j e", j=2)
    ps_xa = bank[4][0:AROWS, 0:SEQ]
    ps_rank = bank[5][:, 0:2 * EXPERTS].rearrange("p (j e) -> p j e", j=2)
    ps_count = bank[6][:, 0:EXPERTS]
    ps_h = [bank[0], bank[1]]
    ps_it = bank[3]
    ps_o = [bank[4], bank[6]]

    S = nc.alloc_semaphore
    const_in, ident_in, wg_in, idx_in, scal_in = S("const_in"), S("ident_in"), S("wg_in"), S("idx_in"), S("scal_in")
    wt_in = [S(f"wt_in{k}") for k in range(KD)]
    upper_in = S("upper_in")
    x_in = [S("x_in0"), S("x_in1")]
    a_in, b_in = S("a_in"), S("b_in")
    wi_in, wo_in = [S("wi_in0"), S("wi_in1")], [S("wo_in0"), S("wo_in1")]
    y_stored = [S("y_stored0"), S("y_stored1")]
    out_is_x, out_pad, y_pad, slots_empty = S("out_is_x"), S("out_pad"), S("y_pad"), S("slots_empty")
    entry_out = [S(f"entry_out{i}") for i in range(2 * TOP)]
    g_list_in, s_list_in = [S("g_list_in0"), S("g_list_in1")], [S("s_list_in0"), S("s_list_in1")]
    yg_in = [S("yg_in0"), S("yg_in1")]
    added = S("added")
    wait_carried = S("wait_carried")
    setup_done, dve_chain, scal_done = S("setup_done"), S("dve_chain"), S("scal_done")
    wt_hi_done, wt_lo_done = S("wt_hi_done"), S("wt_lo_done")
    x_hi_done, x_lo_done = S("x_hi_done"), S("x_lo_done")
    a_hi_done, a_lo_done, b_hi_done, b_lo_done = S("a_hi_done"), S("a_lo_done"), S("b_hi_done"), S("b_lo_done")
    xa_done, xa_hi_done, xa_lo_done = S("xa_done"), S("xa_hi_done"), S("xa_lo_done")
    y_done, y_copied, yt_done, yt_copied = S("y_done"), S("y_copied"), S("yt_done"), S("yt_copied")
    logits_done, gap_done, gap_exp_done, chosen_done = S("logits_done"), S("gap_done"), S("gap_exp_done"), S("chosen_done")
    rank_done, entry_done, count_done, tables_done = S("rank_done"), S("entry_done"), S("count_done"), S("tables_done")
    w_hi_done, w_lo_dve, w_lo_pool = S("w_hi_done"), S("w_lo_dve"), S("w_lo_pool")
    t_yt, t_yt_hi, t_yt_lo = S("t_yt"), S("t_yt_hi"), S("t_yt_lo")
    t_up, t_silu, t_inter = S("t_up"), S("t_silu"), S("t_inter")
    t_it, t_it_hi, t_it_lo = S("t_it"), S("t_it_hi"), S("t_it_lo")
    t_down, t_scaled = S("t_down"), S("t_scaled")

    def steady(engine, body):
        body(0, 0)
        body(1, 1)
        with engine.Fori(1, BATCHES // 2 - 1) as q:
            body(q * 2, 0)
            body(q * 2 + 1, 1)
        body(BATCHES - 2, 0)
        body(BATCHES - 1, 1)

    def known(b):
        return isinstance(b, int)

    def first(b):
        return known(b) and b == 0

    def last(b):
        return known(b) and b == BATCHES - 1

    T0, T1 = 4, TILES - 1
    assert (T1 - T0) % 2 == 0

    def steps(engine, body, before_loop=range(-4, T0), after_loop=range(T1, TILES + 4)):
        for t in before_loop:
            body(t, t % 2, lambda i: 0 <= i < TILES)
        with engine.Fori(T0 // 2, (T1 + 1) // 2) as q:
            body(q * 2, 0, lambda i: True)
            body(q * 2 + 1, 1, lambda i: True)
        for t in after_loop:
            body(t, t % 2, lambda i: 0 <= i < TILES)

    def ok(i, live):
        return live(i) if isinstance(i, int) else True

    def uses(t, d, par):
        return (t - par) * 8 + 16 * ((par + d) // 2 + 1)

    def arrivals(b, par):
        return (b - par) * 8 + 16

    def one(w, e, i, n=1):
        w, i = (w[0], i) if i < KD else (w[1], i - KD)
        if not known(e):
            return w[:, bass.ds(e, 1), i:i + n].rearrange("p e i n -> p (e i n)")
        return w[:, e, i:i + n].rearrange("p i n -> p (i n)")

    block = nc.Block()
    with block:

        @block.sync
        def _(sp):
            def load_x(b, par):
                src = xT[b] if known(b) else xT[bass.ds(b, 1)].rearrange("b p k n -> (b p) k n")
                sp.dma_start(x_raw[:, par], src).then_inc(x_in[par], 16)

            def adapter_of(b):
                i = slice(b, b + 1) if known(b) else bass.ds(b, 1)
                return sp.value_load(adapter_b[0:1, i], min_val=0, max_val=ADAPTERS - 1)

            def load_a(a):
                sp.dma_start(a_raw[:], aT[bass.ds(a, 1)].rearrange("a p g r -> (a p) g r")).then_inc(a_in, 16)

            def load_b(a):
                sp.dma_start(b_raw[:], bT[bass.ds(a, 1)].rearrange("a p n -> (a p) n")).then_inc(b_in, 16)

            def load_expert(e, par, part):
                src, sem, i, n = ((wi, wi_in, 0, KD), (wo, wo_in, KD, KM))[part]
                src = src[e] if known(e) else src[bass.ds(e, 1)].rearrange("e p n -> (e p) n")
                sp.dma_start(one(w_raw, e, i, n), src).then_inc(sem[par], 16)

            def store_y(b, j):
                r = b * SEQ + j * P
                dst = y_rows[r:r + P, :] if known(b) else y_rows[bass.ds(sp.snap(r), P), :]
                sp.wait_ge(y_copied, b * 2 + j + 1)
                sp.dma_start(dst, y_sb[:, j]).then_inc(y_stored[j], 16)

            load_x(0, 0)
            for k in range(KD):
                sp.dma_start(wt_raw[:, k], wT[:, k]).then_inc(wt_in[k], 16)
            sp.wait_ge(idx_in, 16)
            a = adapter_of(0)
            load_a(a)
            load_b(a)

            def batch(b, par):
                if not last(b):
                    a = adapter_of(b + 1)
                    if not first(b):
                        sp.wait_ge(y_done, b * 2)
                    load_x(b + 1, 1 - par)
                    sp.wait_ge(a_lo_done, b + 1)
                    load_a(a)
                if not first(b):
                    store_y(b - 1, 1)
                if not last(b):
                    sp.wait_ge(b_lo_done, b + 1)
                    load_b(a)
                weights = not (known(b) and b >= EXPERTS - 2)
                if first(b):
                    load_expert(b, par, 0)
                    load_expert(b, par, 1)
                if weights:
                    load_expert(b + 1, 1 - par, 0)
                store_y(b, 0)
                if weights:
                    load_expert(b + 1, 1 - par, 1)
                rows = slice(b * SEQ, (b + 1) * SEQ) if known(b) else bass.ds(b * SEQ, SEQ)
                sp.dma_start(out[rows, :], x[rows, :]).then_inc(out_is_x, 16)

            steady(sp, batch)
            e = EXPERTS - 1
            sp.wait_ge(y_done, 2 * BATCHES)
            load_expert(e, e % 2, 0)
            store_y(BATCHES - 1, 1)
            sp.wait_ge(logits_done, 2 * BATCHES)
            for j in range(2):
                sp.wait_ge(y_stored[j], 16 * BATCHES)
            load_expert(e, e % 2, 1)

            sp.wait_ge(tables_done, 1)
            for i in range(2 * TOP):
                sp.wait_ge(entry_out[i], 16 * BATCHES)
            sp.wait_ge(slots_empty, 16)

            def load_list(t, d, ring, sem, par):
                i = t + d
                if isinstance(t, int):
                    row = sp.value_load(block_i[0:1, i:i + 1], min_val=0, max_val=ALL_BLOCKS - 1)
                else:
                    row = sp.value_load(block_i[0:1, bass.ds(i, 1)], min_val=0, max_val=ALL_BLOCKS - 1)
                s = (par + d) % 2
                sp.dma_start(ring[:, s], slots[bass.ds(row * P, P), :]).then_inc(sem[s], 16)

            def step(t, par, live):
                if ok(t + 4, live) if isinstance(t, int) else True:
                    i = t + 4
                    if not (isinstance(i, int) and i < 2):
                        sp.wait_ge(yg_in[par], uses(t, 2, par))
                    load_list(t, 4, g_list, g_list_in, par)
                if ok(t - 1, live):
                    if not (isinstance(t, int) and t - 3 < 0):
                        sp.wait_ge(added, (t - 2) * 16)
                    load_list(t, -1, s_list, s_list_in, par)

            def step_in_loop(t, par, live):
                step(t, par, live)
            for t in range(-4, T0):
                step(t, t % 2, lambda i: 0 <= i < TILES)
            with sp.Fori(T0 // 2, (TILES - 5) // 2) as q:
                step(q * 2, 0, lambda i: True)
                step(q * 2 + 1, 1, lambda i: True)
            for t in range((TILES - 5) // 2 * 2, TILES + 4):
                step(t, t % 2, lambda i: 0 <= i < TILES)
            sp.wait_ge(added, 16 * TILES)

        @block.scalar
        def _(act):
            act.dma_start(adapter_b[:], adapter.partition_broadcast(AROWS)).then_inc(idx_in, 16)
            act.dma_start(smallc[:], consts[:, C_EXPERT:C_ALL]).then_inc(const_in, 16)

            def split_x(b, par):
                act.wait_ge(x_in[par], arrivals(b, par))
                nc.scalar.copy(x_hi[:, par], x_raw[:, par]).then_inc(x_hi_done, 1)

            def split_a(b):
                act.wait_ge(a_in, (b + 1) * 16)
                if not first(b):
                    act.wait_ge(xa_done, b)
                nc.scalar.copy(a_hl[:, :, 0, :], a_raw[:])
                nc.scalar.copy(a_h0[:, :, 0, :], a_raw[:]).then_inc(a_hi_done, 1)

            def split_pair(e, i):
                nc.scalar.copy(one(w_hi, e, 2 * i, 2), one(w_raw, e, 2 * i, 2)).then_inc(w_hi_done, 1)

            def copy_y(b, j):
                act.wait_ge(y_done, b * 2 + j + 1)
                if not first(b):
                    act.wait_ge(yt_done, (b - 1) * 2 + j + 1)
                    act.wait_ge(y_stored[j], b * 16)
                nc.scalar.copy(y_sb[:, j], ps_y[j][:]).then_inc(y_copied, 1)

            split_x(0, 0)
            for k in range(KD):
                act.wait_ge(wt_in[k], 16)
                nc.scalar.copy(wt_hi[:, k], wt_raw[:, k]).then_inc(wt_hi_done, 1)
            act.wait_ge(setup_done, 1)
            split_a(0)
            act.wait_ge(scal_done, 1)

            def batch(b, par):
                if not first(b):
                    copy_y(b - 1, 1)
                act.wait_ge(b_in, (b + 1) * 16)
                if not first(b):
                    act.wait_ge(y_done, b * 2)
                nc.scalar.copy(b_st[:], b_raw[:]).then_inc(b_hi_done, 1)
                act.wait_ge(xa_done, b + 1)
                sc = scal[:, b:b + 1] if known(b) else scal[:, bass.ds(b, 1)]
                nc.scalar.activation(xa_st[:], ps_xa, ACT.Copy, scale=sc).then_inc(xa_hi_done, 1)
                if not (known(b) and b < 2):
                    exp_gap(b - 2)
                weights = not (known(b) and b >= EXPERTS - 1)
                if weights:
                    act.wait_ge(wi_in[par], arrivals(b, par))
                    split_pair(b, 0)
                    split_pair(b, 1)
                if not last(b):
                    split_x(b + 1, 1 - par)
                    split_a(b + 1)
                copy_y(b, 0)
                if weights:
                    act.wait_ge(wo_in[par], arrivals(b, par))
                    split_pair(b, 2)

            def exp_gap(b):
                act.wait_ge(gap_done, b + 1)
                nc.scalar.activation(gap_exp[:], gap[:], ACT.Exp).then_inc(gap_exp_done, 1)

            steady(act, batch)
            exp_gap(BATCHES - 2)
            copy_y(BATCHES - 1, 1)
            e = EXPERTS - 1
            act.wait_ge(wi_in[e % 2], arrivals(e, e % 2))
            split_pair(e, 0)
            split_pair(e, 1)
            exp_gap(BATCHES - 1)
            act.wait_ge(wo_in[e % 2], arrivals(e, e % 2))
            split_pair(e, 2)

            def step(t, par, live):
                if ok(t - 1, live):
                    act.wait_ge(t_up, t)
                    if not (isinstance(t, int) and t - 1 < 1):
                        act.wait_ge(t_it, t - 1)
                    nc.scalar.activation(inter[:], ps_h[(par + 1) % 2][:, 0:M], ACT.Silu).then_inc(t_silu, 1)
                if ok(t + 1, live):
                    act.wait_ge(t_yt, t + 2)
                    if not (isinstance(t, int) and t < 1):
                        act.wait_ge(t_up, t)
                    nc.scalar.copy(yt_hi[:, (par + 1) % 2], ps_yt[:].rearrange("p (k n) -> p k n", k=KD)).then_inc(t_yt_hi, 1)
                if ok(t - 3, live):
                    s = (par + 1) % 2
                    act.wait_ge(t_down, t - 2)
                    act.wait_ge(s_list_in[s], uses(t, -3, par))
                    if not (isinstance(t, int) and t - 3 < 2):
                        act.wait_ge(added, (t - 4) * 16)
                    nc.scalar.activation(scaled[:, s], ps_o[s][:], ACT.Copy,
                                         scale=s_list[:, s, 1:2].bitcast(F32)).then_inc(t_scaled, 1)
                if ok(t - 1, live):
                    act.wait_ge(t_it, t)
                    if not (isinstance(t, int) and t - 1 < 2):
                        act.wait_ge(t_down, t - 2)
                    nc.scalar.copy(it_hi[:, (par + 1) % 2], ps_it[:, 0:M].rearrange("p (k n) -> p k n", k=KM)).then_inc(t_it_hi, 1)

            steps(act, step)

        @block.vector
        def _(dve):
            chained = [0]

            def chain(ins):
                chained[0] += 1
                ins.then_inc(dve_chain, 1)
                dve.wait_ge(dve_chain, chained[0])

            V = nc.vector
            V.memset(a_h0[:].bitcast(F32), 0.0)
            V.memset(before[:], 0.0)
            V.memset(one8[:], 1.0)
            V.memset(ones[:], 1.0).then_inc(setup_done, 1)
            dve.wait_ge(idx_in, 16)
            dve.wait_ge(scal_in, 16)
            dve.wait_ge(const_in, 16)
            chain(V.tensor_copy(adapter_f[:], adapter_b[:]))
            chain(V.tensor_tensor(scal_oh[:], adapter_f[:].unsqueeze(2).to_broadcast([AROWS, BATCHES, ADAPTERS]),
                                  expert_no[0:AROWS].unsqueeze(1).to_broadcast([AROWS, BATCHES, ADAPTERS]), ALU.is_equal))
            chain(V.tensor_tensor(scal_oh[:], scal_oh[:], scal_b[:].unsqueeze(1).to_broadcast([AROWS, BATCHES, ADAPTERS]), ALU.mult))
            V.tensor_reduce(scal[:], scal_oh[:], AX.X, ALU.add).then_inc(scal_done, 1)

            def low(out, raw, high):
                return V.tensor_tensor(out, raw, high.bitcast(F32), ALU.subtract)

            def split_x(b, par):
                dve.wait_ge(x_hi_done, b + 1)
                low(x_lo[:, par], x_raw[:, par], x_hi[:, par]).then_inc(x_lo_done, 1)

            def split_a(b):
                dve.wait_ge(a_hi_done, b + 1)
                low(a_hl[:, :, 1, :], a_raw[:], a_hl[:, :, 0, :]).then_inc(a_lo_done, 1)

            split_x(0, 0)
            for k in range(KD):
                dve.wait_ge(wt_hi_done, k + 1)
                low(wt_lo[:, k], wt_raw[:, k], wt_hi[:, k]).then_inc(wt_lo_done, 1)
            split_a(0)
            dve.wait_ge(upper_in, 16)
            V.tensor_copy(upper[:], upper_raw[:]).then_inc(setup_done, 1)

            def copy_yt(b, j):
                dve.wait_ge(yt_done, b * 2 + j + 1)
                if not first(b):
                    dve.wait_ge(logits_done, (b - 1) * 2 + j + 1)
                V.tensor_copy(yt_sb[:, j], ps_yt[:].rearrange("p (k n) -> p k n", k=KD)).then_inc(yt_copied, 1)

            ROUTE = 12

            class link:
                def __init__(self, b):
                    self.b, self.n = b, 0

                def __call__(self, ins, wait=True):
                    self.n += 1
                    ins.then_inc(dve_chain, 1)
                    if wait:
                        dve.wait_ge(dve_chain, self.b * ROUTE + (SETUP + self.n))

                def skip(self):
                    dve.wait_ge(dve_chain, self.b * ROUTE + (SETUP + self.n))

            SETUP = chained[0]

            def choose(b, par, ln):
                dve.wait_ge(logits_done, (b + 1) * 2)
                V.tensor_scalar(token_no, token_no, float(SEQ), None, ALU.add)
                V.max(best[:, 0], ps_log[:, 0])
                ln(V.max(best[:, 1], ps_log[:, 1]))
                V.tensor_tensor(gap[:], best[:, :, 1], best[:, :, 0], ALU.subtract).then_inc(gap_done, 1)
                V.max_index(best_at[:, 0], best[:, 0], ps_log[:, 0])
                ln(V.max_index(best_at[:, 1], best[:, 1], ps_log[:, 1]))
                ln(V.tensor_copy(best_f[:], best_at[:, :, 0:TOP]))
                shape = [P, 2 * TOP, EXPERTS]
                ln(V.tensor_tensor(onehot[:].rearrange("p j k e -> p (j k) e"),
                                   best_f[:].rearrange("p j k -> p (j k)").unsqueeze(2).to_broadcast(shape),
                                   expert_no.unsqueeze(1).to_broadcast(shape), ALU.is_equal))
                if not first(b):
                    dve.wait_ge(rank_done, b)
                ln(V.tensor_tensor(chosen[:], onehot[:, :, 0], onehot[:, :, 1], ALU.add))
                ln(V.tensor_tensor(before[:, 1 - par], before[:, par], chosen[:, 0], ALU.add))
                V.tensor_tensor(before[:, 1 - par], before[:, 1 - par], chosen[:, 1], ALU.add).then_inc(chosen_done, 1)

            def weigh(b, ln):
                dve.wait_ge(gap_exp_done, b + 1)
                if not first(b):
                    for i in range(2 * TOP):
                        dve.wait_ge(entry_out[i], b * 16)
                e = entry[:].bitcast(F32).rearrange("p (j k) c -> p j k c", j=2)
                ln(V.tensor_scalar(gap_den[:], gap_exp[:], 1.0, None, ALU.add))
                ln(V.reciprocal(e[:, :, 0, 1], gap_den[:]))
                V.tensor_tensor(e[:, :, 1, 1], gap_exp[:], e[:, :, 0, 1], ALU.mult)
                ln(V.tensor_copy(entry[:, :, 0], token_no))

            def place(b, ln):
                dve.wait_ge(rank_done, b + 1)
                ln(V.tensor_tensor(row_of[:], ps_rank, base_row.unsqueeze(1).to_broadcast([P, 2, EXPERTS]), ALU.add))
                for k in range(TOP):
                    final = V.tensor_tensor(row_oh[:, :, k], onehot[:, :, k], row_of[:], ALU.mult)
                ln(final)
                ln(V.tensor_reduce(row_f[:], row_oh[:].rearrange("p j k e -> p (j k) e"), AX.X, ALU.add))
                assert ln.n == ROUTE
                V.tensor_copy(row_no[:], row_f[:]).then_inc(entry_done, 1)

            def split_odd(e, i):
                dve.wait_ge(w_hi_done, e * PAIRS + i + 1)
                low(one(w_lo, e, 2 * i + 1), one(w_raw, e, 2 * i + 1), one(w_hi, e, 2 * i + 1)).then_inc(w_lo_dve, 1)

            def batch(b, par):
                if not first(b):
                    copy_yt(b - 1, 0)
                third = 2 * RANK
                dve.wait_ge(b_hi_done, b + 1)
                low(b_st[2 * third:], b_raw[2 * third:], b_st[2 * third:]).then_inc(b_lo_done, 1)
                dve.wait_ge(xa_hi_done, b + 1)
                sc = scal[third:2 * third, b:b + 1] if known(b) else scal[third:2 * third, bass.ds(b, 1)]
                V.scalar_tensor_tensor(xa_st[third:2 * third], ps_xa[third:2 * third], sc, xa_st[third:2 * third].bitcast(F32),
                                       ALU.mult, ALU.subtract).then_inc(xa_lo_done, 1)
                two = not (known(b) and b < 2)
                weights = not (known(b) and b >= EXPERTS - 1)
                ln = link(b - 2) if two else None
                if two:
                    choose(b - 2, par, ln)
                if weights:
                    split_odd(b, 0)
                if not last(b):
                    split_x(b + 1, 1 - par)
                    split_a(b + 1)
                if not first(b):
                    copy_yt(b - 1, 1)
                if two:
                    weigh(b - 2, ln)
                    place(b - 2, ln)
                if weights:
                    split_odd(b, 1)
                    split_odd(b, 2)

            steady(dve, batch)
            b = BATCHES - 1
            ln = link(b - 1)
            choose(b - 1, 0, ln)
            copy_yt(b, 0)
            copy_yt(b, 1)
            weigh(b - 1, ln)
            place(b - 1, ln)
            ln = link(b)
            choose(b, 1, ln)
            weigh(b, ln)
            place(b, ln)
            chained[0] = SETUP + ROUTE * BATCHES
            dve.wait_ge(count_done, 1)
            shape = [1, EXPERTS, BLOCKS]
            chain(V.tensor_tensor(cmp_n[:], ps_count[0:1].unsqueeze(2).to_broadcast(shape),
                                  thresholds.unsqueeze(1).to_broadcast(shape), ALU.is_gt))
            chain(V.tensor_reduce(n_tiles[:], cmp_n[:], AX.X, ALU.add))
            chain(V.tensor_tensor_scan(tile_end[:], one8[:], n_tiles[:], 0.0, ALU.mult, ALU.add))
            shape = [1, TILES, EXPERTS - 1]
            chain(V.tensor_tensor(cmp_t[:], tile_no.unsqueeze(2).to_broadcast(shape),
                                  tile_end[:, 0:EXPERTS - 1].unsqueeze(1).to_broadcast(shape), ALU.is_ge))
            V.tensor_tensor(cmp_s[:], cmp_t[:], n_tiles[:, 0:EXPERTS - 1].unsqueeze(1).to_broadcast(shape), ALU.mult)
            chain(V.tensor_reduce(expert_f[:], cmp_t[:], AX.X, ALU.add))
            chain(V.tensor_reduce(start_f[:], cmp_s[:], AX.X, ALU.add))
            V.tensor_copy(expert_i[:], expert_f[:])
            chain(V.scalar_tensor_tensor(block_f[:], expert_f[:], float(BLOCKS), tile_no, ALU.mult, ALU.add))
            V.tensor_tensor(block_i[:], block_f[:], start_f[:], ALU.subtract).then_inc(tables_done, 1)
            for i in range(PAIRS):
                split_odd(EXPERTS - 1, i)

            def step(t, par, live):
                if ok(t - 1, live):
                    dve.wait_ge(t_silu, t)
                    V.tensor_tensor(inter[:], inter[:], ps_h[(par + 1) % 2][:, M:2 * M], ALU.mult).then_inc(t_inter, 1)
                if ok(t + 1, live):
                    dve.wait_ge(t_yt_hi, t + 2)
                    s = (par + 1) % 2
                    low(yt_lo[:, s], ps_yt[:].rearrange("p (k n) -> p k n", k=KD), yt_hi[:, s]).then_inc(t_yt_lo, 1)
                if ok(t - 1, live):
                    dve.wait_ge(t_it_hi, t)
                    s = (par + 1) % 2
                    low(it_lo[:, s], ps_it[:, 0:M].rearrange("p (k n) -> p k n", k=KM), it_hi[:, s]).then_inc(t_it_lo, 1)

            steps(dve, step)

        @block.gpsimd
        def _(pool):
            pool.dma_start(scal_b[:], scalings.partition_broadcast(AROWS)).then_inc(scal_in, 16)
            pool.dma_start(ident[:], consts[:, C_IDENT:C_IDENT + P]).then_inc(ident_in, 16)
            pool.dma_start(wg[:], w_gate).then_inc(wg_in, 16)
            pool.dma_start(upper_raw[:], consts[:, C_UPPER:C_UPPER + P]).then_inc(upper_in, 16)
            pool.dma_start(slots, empty_list).then_inc(slots_empty, 16)
            pool.dma_start(out[TOKENS:TOKENS + P], zeros).then_inc(out_pad, 16)
            pool.dma_start(y_rows[TOKENS:TOKENS + P], zeros).then_inc(y_pad, 16)

            def carry_wait():
                pool.sem_inc(wait_carried, 1)

            pool.wait_ge(slots_empty, 16)

            def split_even(e, i):
                pool.wait_ge(w_hi_done, e * PAIRS + i + 1)
                nc.gpsimd.tensor_tensor(one(w_lo, e, 2 * i), one(w_raw, e, 2 * i), one(w_hi, e, 2 * i).bitcast(F32),
                                        ALU.subtract).then_inc(w_lo_pool, 1)

            def list_entries(b):
                pool.wait_ge(entry_done, b + 1)
                carry_wait()
                for i in range(2 * TOP):
                    pool.indirect_dma_start(slots, bass.IndirectOffsetOnAxis(row_no[:, i:i + 1], 0), entry[:, i], None).then_inc(entry_out[i], 16)

            def batch(b, par):
                if not (known(b) and b >= EXPERTS - 1):
                    for i in range(PAIRS):
                        split_even(b, i)
                if not (known(b) and b < 2):
                    list_entries(b - 2)

            steady(pool, batch)
            list_entries(BATCHES - 2)
            split_even(EXPERTS - 1, 0)
            split_even(EXPERTS - 1, 1)
            list_entries(BATCHES - 1)
            split_even(EXPERTS - 1, 2)
            for j in range(2):
                pool.wait_ge(y_stored[j], 16 * BATCHES)
            pool.wait_ge(y_pad, 16)
            pool.wait_ge(out_pad, 16)
            pool.wait_ge(out_is_x, 16 * BATCHES)

            def step(t, par, live):
                if ok(t + 2, live):
                    pool.wait_ge(g_list_in[par], uses(t, 2, par))
                    if not (isinstance(t, int) and t < 0):
                        pool.wait_ge(t_yt, t + 1)
                    carry_wait()
                    pool.indirect_dma_start(yg[:, par], None, y_rows, bass.IndirectOffsetOnAxis(g_list[:, par, 0:1], 0)).then_inc(yg_in[par], 16)
                if ok(t - 3, live):
                    s = (par + 1) % 2
                    pool.wait_ge(t_scaled, t - 2)
                    if not (isinstance(t, int) and t - 3 < 1):
                        pool.wait_ge(added, (t - 3) * 16)
                    carry_wait()
                    pool.indirect_dma_start(out, bass.IndirectOffsetOnAxis(s_list[:, s, 0:1], 0), scaled[:, s], None,
                                            compute_op=ALU.add).then_inc(added, 16)

            for t in range(-4, T0):
                step(t, t % 2, lambda i: 0 <= i < TILES)
            with pool.Fori(T0 // 2, (TILES - 3) // 2) as q:
                step(q * 2, 0, lambda i: True)
                step(q * 2 + 1, 1, lambda i: True)
            for t in range((TILES - 3) // 2 * 2, TILES + 4):
                step(t, t % 2, lambda i: 0 <= i < TILES)

        @block.tensor
        def _(pe):
            mm = nc.tensor.matmul

            def adapter_in(b, par):
                pe.wait_ge(x_lo_done, b + 1)
                pe.wait_ge(a_lo_done, b + 1)
                if not first(b):
                    pe.wait_ge(xa_lo_done, b)
                for k in range(KD):
                    mm(ps_xa, a_hl[:, k * GROUPS:(k + 1) * GROUPS].rearrange("p g c r -> p (g c r)"), x_hi[:, par, k], start=(k == 0), stop=False)
                    final = mm(ps_xa, a_h0[:, k * GROUPS:(k + 1) * GROUPS].rearrange("p g c r -> p (g c r)"), x_lo[:, par, k], start=False, stop=(k == KD - 1))
                final.then_inc(xa_done, 1)

            def base(b, par, j):
                if not first(b):
                    pe.wait_ge(y_copied, (b - 1) * 2 + j + 1)
                elif j == 0:
                    pe.wait_ge(x_lo_done, 1)
                cols = slice(j * P, (j + 1) * P)
                for k in range(KD):
                    if known(b) and b == 0 and j == 0:
                        pe.wait_ge(wt_lo_done, k + 1)
                    mm(ps_y[j][:], x_hi[:, par, k, cols], wt_hi[:, k], start=(k == 0), stop=False)
                    mm(ps_y[j][:], x_hi[:, par, k, cols], wt_lo[:, k], start=False, stop=False)
                    mm(ps_y[j][:], x_lo[:, par, k, cols], wt_hi[:, k], start=False, stop=False)

            def delta(b, j):
                if j == 0:
                    pe.wait_ge(xa_lo_done, b + 1)
                    pe.wait_ge(b_lo_done, b + 1)
                mm(ps_y[j][:], xa_st[:, j * P:(j + 1) * P], b_st[:], start=False, stop=True).then_inc(y_done, 1)

            def turn_y(b, j):
                pe.wait_ge(y_copied, b * 2 + j + 1)
                if j == 1:
                    pe.wait_ge(yt_copied, b * 2 + 1)
                elif not first(b):
                    pe.wait_ge(yt_copied, b * 2)
                for k in range(KD):
                    final = nc.tensor.transpose(ps_yt[:, k * P:(k + 1) * P], y_sb[:, j, k * P:(k + 1) * P], ident[:])
                final.then_inc(yt_done, 1)

            def logits(b, j):
                pe.wait_ge(yt_copied, b * 2 + j + 1)
                if j == 0 and not first(b):
                    pe.wait_ge(chosen_done, b)
                for k in range(KD):
                    final = mm(ps_log[:, j], yt_sb[:, j, k], wg[:, k], start=(k == 0), stop=(k == KD - 1))
                final.then_inc(logits_done, 1)

            def rank(b, par):
                pe.wait_ge(chosen_done, b + 1)
                if not first(b):
                    pe.wait_ge(entry_done, b)
                mm(ps_rank[:, 0], upper[:], chosen[:, 0], start=True, stop=False)
                mm(ps_rank[:, 0], ones[:], before[:, par], start=False, stop=True)
                mm(ps_rank[:, 1], upper[:], chosen[:, 1], start=True, stop=False)
                mm(ps_rank[:, 1], ones[:], chosen[:, 0], start=False, stop=False)
                mm(ps_rank[:, 1], ones[:], before[:, par], start=False, stop=True).then_inc(rank_done, 1)

            def batch(b, par):
                after_one, two = not first(b), not (known(b) and b < 2)
                if not first(b):
                    adapter_in(b, par)
                base(b, par, 0)
                if first(b):
                    adapter_in(b, par)
                if after_one:
                    logits(b - 1, 0)
                if two:
                    rank(b - 2, par)
                if after_one:
                    turn_y(b - 1, 1)
                delta(b, 0)
                base(b, par, 1)
                if after_one:
                    logits(b - 1, 1)
                else:
                    pe.wait_ge(ident_in, 16)
                    pe.wait_ge(wg_in, 16)
                    pe.wait_ge(setup_done, 2)
                turn_y(b, 0)
                delta(b, 1)

            steady(pe, batch)
            b = BATCHES - 1
            rank(b - 1, 0)
            logits(b, 0)
            turn_y(b, 1)
            logits(b, 1)
            rank(b, 1)
            mm(ps_count, ones[:], before[:, 0], start=True, stop=True).then_inc(count_done, 1)

            pe.wait_ge(w_lo_pool, PAIRS * EXPERTS)
            pe.wait_ge(w_lo_dve, PAIRS * EXPERTS)
            pe.wait_ge(tables_done, 1)
            pe.wait_ge(yt_copied, 2 * BATCHES)
            pe.wait_ge(entry_done, BATCHES)

            def step(t, par, live):
                nxt = (par + 1) % 2
                if ok(t + 1, live):
                    pe.wait_ge(yg_in[nxt], uses(t, 1, par))
                    if not (isinstance(t, int) and t + 1 < 1):
                        pe.wait_ge(t_yt_lo, t + 1)
                    for k in range(KD):
                        final = nc.tensor.transpose(ps_yt[:, k * P:(k + 1) * P], yg[:, nxt, k * P:(k + 1) * P], ident[:])
                    final.then_inc(t_yt, 1)
                if ok(t, live):
                    i = slice(t, t + 1) if isinstance(t, int) else bass.ds(t, 1)
                    e = pe.value_load(expert_i[0:1, i], min_val=0, max_val=EXPERTS - 1)
                    pe.wait_ge(t_yt_lo, t + 1)
                    if not (isinstance(t, int) and t < 2):
                        pe.wait_ge(t_inter, t - 1)
                    h = ps_h[par][:]
                    for k in range(KD):
                        hi = one(w_hi, e, k)
                        lo = one(w_lo, e, k)
                        mm(h, yt_hi[:, par, k], hi, start=(k == 0), stop=False)
                        mm(h, yt_lo[:, par, k], hi, start=False, stop=False)
                        final = mm(h, yt_hi[:, par, k], lo, start=False, stop=(k == KD - 1))
                    final.then_inc(t_up, 1)
                if ok(t - 1, live):
                    pe.wait_ge(t_inter, t)
                    if not (isinstance(t, int) and t - 1 < 1):
                        pe.wait_ge(t_it_lo, t - 1)
                    for k in range(KM):
                        final = nc.tensor.transpose(ps_it[:, k * P:(k + 1) * P], inter[:, k * P:(k + 1) * P], ident[:])
                    final.then_inc(t_it, 1)
                if ok(t - 2, live):
                    i = slice(t - 2, t - 1) if isinstance(t, int) else bass.ds(t - 2, 1)
                    e = pe.value_load(expert_i[0:1, i], min_val=0, max_val=EXPERTS - 1)
                    pe.wait_ge(t_it_lo, t - 1)
                    if not (isinstance(t, int) and t - 2 < 2):
                        pe.wait_ge(t_scaled, t - 3)
                    o = ps_o[par][:]
                    for k in range(KM):
                        hi = one(w_hi, e, KD + k)
                        lo = one(w_lo, e, KD + k)
                        mm(o, it_hi[:, par, k], hi, start=(k == 0), stop=False)
                        mm(o, it_lo[:, par, k], hi, start=False, stop=False)
                        final = mm(o, it_hi[:, par, k], lo, start=False, stop=(k == KM - 1))
                    final.then_inc(t_down, 1)

            steps(pe, step)


def kernel(**inputs):
    import concourse.bacc as bacc
    from concourse.bass_utils import run_bass_kernel_spmd as run

    n = {k: np.asarray(v) for k, v in inputs.items()}
    x = np.ascontiguousarray(n["x"].reshape(TOKENS, D))
    consts, empty_list, zeros = constants()
    wi = np.concatenate([n["L0_ffn_wi_0"], n["L0_ffn_wi_1"]], axis=2).reshape(EXPERTS, KD, P, 2 * M)
    wo = n["L0_ffn_wo"].reshape(EXPERTS, KM, P, D)
    a = n["L0_cond_A"].reshape(ADAPTERS, RANK, KD, 1, P).transpose(0, 4, 2, 3, 1)
    a = np.tile(a, (1, 1, 1, GROUPS, 1)).reshape(ADAPTERS, P, KD * GROUPS, RANK)
    b = np.tile(n["L0_cond_Bm"].transpose(0, 2, 1), (1, 2 * GROUPS, 1))
    arrays = {
        "xT": x.reshape(BATCHES, SEQ, KD, P).transpose(0, 3, 2, 1),
        "x": x,
        "wT": n["L0_cond_W"].T.reshape(KD, P, D).transpose(1, 0, 2),
        "aT": a,
        "bT": b,
        "scalings": n["L0_cond_scalings"],
        "adapter": n["itok_B_0_6"],
        "w_gate": n["L0_ffn_w_gate"].reshape(KD, P, EXPERTS).transpose(1, 0, 2),
        "wi": wi.transpose(0, 2, 1, 3).reshape(EXPERTS, P, KD * D),
        "wo": wo.transpose(0, 2, 1, 3).reshape(EXPERTS, P, KM * D),
        "consts": consts,
        "empty_list": empty_list,
        "zeros": zeros,
    }
    nc = bacc.Bacc("TRN2", target_bir_lowering=False, num_devices=1, dynamic_dma_scratch_size=SCRATCH)
    given, aps = {}, {}
    for name, v in arrays.items():
        v = np.ascontiguousarray(v)
        given[f"in_{name}"] = v
        aps[name] = nc.dram_tensor(f"in_{name}", v.shape, mybir.dt.from_np(v.dtype), kind="ExternalInput").ap()
    out = nc.dram_tensor("out_0", (TOKENS + P, D), F32, kind="ExternalOutput").ap()
    build(nc, out=out, **aps)
    r = run(nc, [given], core_ids=[0])
    return r.results[0]["out_0"][:TOKENS].reshape(BATCHES, SEQ, D)
```

```python
import numpy as np
import concourse.bass as bass
from concourse import mybir
from concourse.alu_op_type import AluOpType as ALU

F32, F32R = mybir.dt.float32, mybir.dt.float32r
BF16, I32, U32 = mybir.dt.bfloat16, mybir.dt.int32, mybir.dt.uint32
ACT = mybir.ActivationFunctionType
AX = mybir.AxisListType

P = 128
BATCHES, SEQ, D = 8, 256, 512
TOKENS = BATCHES * SEQ
HALVES = SEQ // P
KD = D // P
ADAPTERS, RANK = 8, 16
EXPERTS, TOP, M = 8, 2, 256
KM = M // P
GROUPS = 3
AROWS = GROUPS * 2 * RANK
PIECES = KD + KM
PAIRS = PIECES // 2
ROWS = AROWS + 2 * EXPERTS
LATE = EXPERTS - 2
SLOTS = 3
FIRST_LISTS = 4
BLOCKS = TOKENS // P
TILES = TOP * TOKENS // P + EXPERTS - 1
SPARE = EXPERTS - 1
ALL_BLOCKS = SPARE + EXPERTS * BLOCKS
assert TILES - TOP * TOKENS // P >= LATE
SCRATCH = 4096

C_IDENT, C_UPPER, C_EXPERT, C_BASE, C_THR, C_TILE, C_TOK = 0, P, 2 * P, 2 * P + 8, 2 * P + 16, 2 * P + 32, 2 * P + 72
C_GATE, C_ADAPTER, C_SAME = C_TOK + 4, C_TOK + 12, C_TOK + 13
C_ALL = C_SAME + 2 * RANK


def constants():
    c = np.zeros((P, C_ALL), np.float32)
    c[:, C_IDENT:C_IDENT + P] = np.eye(P)
    c[:, C_UPPER:C_UPPER + P] = np.triu(np.ones((P, P)), 1)
    c[:, C_EXPERT:C_EXPERT + EXPERTS] = np.arange(EXPERTS)
    c[:, C_BASE:C_BASE + EXPERTS] = np.arange(EXPERTS) * TOKENS + SPARE * P
    c[:, C_THR:C_THR + BLOCKS] = np.arange(BLOCKS) * P
    c[:, C_TILE:C_TILE + 40] = np.arange(40) - TILES
    c[:, C_TOK:C_TOK + 4] = np.arange(P)[:, None] + np.array([0, 0, P, P]) - SEQ
    c[AROWS:ROWS, C_GATE:C_GATE + EXPERTS] = np.tile(np.eye(EXPERTS), (2, 1))
    c[:, C_ADAPTER] = np.arange(P) // RANK
    c[:, C_SAME:C_ALL] = np.arange(P)[:, None] % RANK == np.arange(2 * RANK) % RANK
    empty = np.zeros((ALL_BLOCKS * P, 2), np.int32)
    empty[:, 0] = TOKENS + np.arange(ALL_BLOCKS * P) % P
    return c, empty, np.zeros((P, D), np.float32)


def build(nc, xT, x, wT, w, aT, bT, b_all, scalings, adapter, w_gate, experts, consts, empty_list, zeros, out):
    y_rows = nc.dram_tensor("y_rows", (TOKENS + P, D), F32).ap()
    slots = nc.dram_tensor("slots", (ALL_BLOCKS * P, 2), I32).ap()

    top = [nc.sbuf_base + (-nc.sbuf_base) % 64]

    def size(shape, dt):
        n = {BF16: 2}.get(dt, 4)
        for s in shape[1:]:
            n *= s
        return n + (-n) % 32

    def put(name, shape, dt, at=None):
        if at is None:
            at = top[0]
            top[0] += size(shape, dt)
        return nc.alloc_sbuf_tensor_at(name, shape, dt, offset=at)

    wi_hi = put("wi_hi", [P, EXPERTS, KD, D], F32R)
    wo_hi = put("wo_hi", [P, EXPERTS, KM, D], F32R)
    wi_lo_at = top[0]
    wi_lo = put("wi_lo", [P, EXPERTS, KD, D], F32R)
    wo_lo_at = top[0]
    wo_lo = put("wo_lo", [P, EXPERTS, KM, D], F32R)
    w_hi, w_lo = (wi_hi, wo_hi), (wi_lo, wo_lo)
    w_raw = (put("wi_raw", [P, EXPERTS, KD, D], F32, wi_lo_at), put("wo_raw", [P, EXPERTS, KM, D], F32, wo_lo_at))

    wi_expert, wo_expert = KD * D * 4, KM * D * 4
    wi_hi_at, wo_hi_at = wi_lo_at - EXPERTS * (wi_expert + wo_expert), wi_lo_at - EXPERTS * wo_expert
    x_hi = put("x_hi", [P, SLOTS, KD, SEQ], F32R, wi_hi_at + LATE * wi_expert)
    x_lo = put("x_lo", [P, SLOTS, KD, SEQ], F32R, wi_lo_at + LATE * wi_expert)
    x_raw = put("x_raw", [P, SLOTS, KD, SEQ], F32, wi_lo_at + LATE * wi_expert)
    wt_hi = put("wt_hi", [P, KD, D], F32R, wo_hi_at + LATE * wo_expert)
    wt_lo = put("wt_lo", [P, KD, D], F32R, wo_lo_at + LATE * wo_expert)
    wt_raw = put("wt_raw", [P, KD, D], F32, wo_lo_at + LATE * wo_expert)
    shared = top[0]
    w_nat = put("w_nat", [P, KD, D], F32, wi_hi_at + (LATE - 1) * wi_expert)
    top[0] = wo_hi_at + (LATE - 1) * wo_expert
    b_nat = put("b_nat", [P, KD, ADAPTERS * RANK], F32)
    select = put("select", [P, BATCHES, 2 * RANK], F32)
    upper_raw = put("upper_raw", [P, P], F32)
    scal_oh = put("scal_oh", [AROWS, BATCHES, ADAPTERS], F32)
    wg = put("wg", [P, KD, EXPERTS], F32)
    mask = put("mask", [P, BATCHES], F32)
    g_all = put("g_all", [P, EXPERTS], F32)
    assert top[0] <= wo_hi_at + LATE * wo_expert
    top[0] = shared

    yg = put("yg", [P, 2, D], F32)
    yt_hi = put("yt_hi", [P, 2, KD, P], F32R)
    yt_lo = put("yt_lo", [P, 2, KD, P], F32R)
    inter = put("inter", [P, M], F32)
    it_hi = put("it_hi", [P, 2, KM, P], F32R)
    it_lo = put("it_lo", [P, 2, KM, P], F32R)
    scaled = put("scaled", [P, 2, D], F32)
    end2 = top[0]
    top[0] = shared
    best = put("best", [P, 2, 8], F32)
    best_at = put("best_at", [P, 2, 8], U32)
    best_f = put("best_f", [P, 2, TOP], F32)
    onehot = put("onehot", [P, 2, TOP, EXPERTS], F32)
    row_of = put("row_of", [P, 2, EXPERTS], F32)
    row_f = put("row_f", [P, 2 * TOP], F32)
    row_oh = put("row_oh", [P, 2, TOP, EXPERTS], F32)
    cmp_n = put("cmp_n", [1, EXPERTS, BLOCKS], F32)
    cmp_t = put("cmp_t", [1, TILES, EXPERTS - 1], F32)
    cmp_s = put("cmp_s", [1, TILES, EXPERTS - 1], F32)
    assert top[0] <= shared + 2 * D * 4
    top[0] = shared + 2 * D * 4
    y_sb = put("y_sb", [P, 2, D], F32)
    a_raw = put("a_raw", [P, KD, GROUPS, RANK], F32)
    b_raw = put("b_raw", [AROWS, D], F32)
    a_hl = put("a_hl", [P, KD, ROWS], F32R)
    a_h0 = put("a_h0", [P, KD, ROWS], F32R)
    b_st = put("b_st", [AROWS, D], F32R)
    xa_st = put("xa_st", [AROWS, SLOTS, SEQ], F32R)
    xl = put("xl", [ROWS, SEQ], F32)
    expert_f = put("expert_f", [1, TILES], F32)
    start_f = put("start_f", [1, TILES], F32)
    block_f = put("block_f", [1, TILES], F32)
    tile_rel = put("tile_rel", [1, TILES], F32)
    top[0] = max(top[0], end2)
    ident = put("ident", [P, P], F32)
    upper = put("upper", [P, P], BF16)
    ones = put("ones", [P, P], BF16)
    smallc = put("smallc", [P, C_ALL - C_EXPERT], F32)

    def const(c, n, rows=P):
        return smallc[0:rows, c - C_EXPERT:c - C_EXPERT + n]

    expert_no, base_row, token_no = const(C_EXPERT, EXPERTS), const(C_BASE, EXPERTS), const(C_TOK, 4)
    thresholds, tile_no = const(C_THR, BLOCKS, 1), const(C_TILE, TILES, 1)
    adapter_b = put("adapter_b", [P, BATCHES], I32)
    adapter_f = put("adapter_f", [P, BATCHES], F32)
    scal_b = put("scal_b", [AROWS, ADAPTERS], F32)
    scal = put("scal", [ROWS, BATCHES], F32)
    gate = put("gate", [ROWS, BATCHES, EXPERTS], F32)
    chosen = put("chosen", [P, 2, EXPERTS], BF16)
    before = put("before", [P, SLOTS, EXPERTS], BF16)
    between = put("between", [P, EXPERTS], BF16)
    gap = put("gap", [P, 2], F32)
    gap_exp = put("gap_exp", [P, 2], F32)
    gap_den = put("gap_den", [P, 2], F32)
    row_no = put("row_no", [P, SLOTS, 2 * TOP], I32)
    entry = put("entry", [P, SLOTS, 2 * TOP, 2], I32)
    n_tiles = put("n_tiles", [1, EXPERTS], F32)
    one8 = put("one8", [1, EXPERTS], F32)
    tile_end = put("tile_end", [1, EXPERTS], F32)
    expert_i = put("expert_i", [1, TILES], I32)
    block_i = put("block_i", [1, TILES], I32)
    g_list = put("g_list", [P, FIRST_LISTS, 2], I32)
    s_list = put("s_list", [P, 2, 2], I32)
    silu_in = put("silu_in", [P, 1], F32)
    assert top[0] <= nc.sbuf_usable_end

    bank = [nc.alloc_psum_tensor(f"bank{i}", [P, 512], F32) for i in range(8)]
    ps_y = [bank[0], bank[1]]
    ps_yt = bank[2]
    ps_log = bank[3][:, 0:2 * EXPERTS].rearrange("p (j e) -> p j e", j=2)
    ps_xa = [bank[4][0:ROWS, 0:SEQ], bank[4][0:ROWS, SEQ:2 * SEQ], bank[7][0:ROWS, SEQ:2 * SEQ]]
    ps_rank = bank[5][:, 0:2 * EXPERTS].rearrange("p (j e) -> p j e", j=2)
    ps_count = bank[6][:, 0:EXPERTS]
    ps_wg = bank[5][:, 0:KD * EXPERTS]
    ps_g = bank[6][:, 0:EXPERTS]
    ps_gate = bank[7][0:2 * RANK, 0:BATCHES * EXPERTS]
    ps_h = [bank[0], bank[1]]
    ps_it = bank[3]
    ps_o = [bank[4], bank[6]]

    S = nc.alloc_semaphore
    const_in, ident_in, wg_in, idx_in, scal_in = S("const_in"), S("ident_in"), S("wg_in"), S("idx_in"), S("scal_in")
    upper_in, w_nat_in, b_nat_in = S("upper_in"), S("w_nat_in"), S("b_nat_in")
    wt_in = [S(f"wt_in{k}") for k in range(KD)]
    x_in = [S(f"x_in{i}") for i in range(SLOTS)]
    a_in, b_in = S("a_in"), S("b_in")
    pairs_in = [[S(f"pair_in{i}_{n}") for n in range(2)] for i in range(SLOTS)]
    late_in = [S(f"late_in{i}") for i in range((EXPERTS - LATE) * PAIRS)]
    y_stored = [S("y_stored0"), S("y_stored1")]
    out_is_x, out_pad = S("out_is_x"), S("out_pad")
    entry_out = [S(f"entry_out{i}") for i in range(SLOTS)]
    g_list_in, s_list_in = [S(f"g_list_in{i}") for i in range(FIRST_LISTS)], [S("s_list_in0"), S("s_list_in1")]
    yg_in = [S("yg_in0"), S("yg_in1")]
    added = S("added")
    wait_carried = S("wait_carried")
    setup_done, dve_chain, scal_done = S("setup_done"), S("dve_chain"), S("scal_done")
    gate_product, gate_copied = S("gate_product"), S("gate_copied")
    w_gate_done, w_gate_hi, w_gate_lo = S("w_gate_done"), S("w_gate_hi"), S("w_gate_lo")
    wt_hi_done, wt_lo_done = S("wt_hi_done"), S("wt_lo_done")
    x_hi_done, x_lo_done = S("x_hi_done"), S("x_lo_done")
    a_hi_done, a_lo_done, b_hi_done, b_lo_done = S("a_hi_done"), S("a_lo_done"), S("b_hi_done"), S("b_lo_done")
    xa_done, xl_done, xa_hi_done, xa_lo_done = S("xa_done"), S("xl_done"), S("xa_hi_done"), S("xa_lo_done")
    y_done, y_copied = S("y_done"), S("y_copied")
    logits_done, gap_done, gap_exp_done, chosen_done = S("logits_done"), S("gap_done"), S("gap_exp_done"), S("chosen_done")
    rank_done, entry_done, count_done, tables_done = S("rank_done"), S("entry_done"), S("count_done"), S("tables_done")
    w_hi_done, w_lo_dve, w_lo_pool = S("w_hi_done"), S("w_lo_dve"), S("w_lo_pool")
    t_yt, t_yt_hi, t_yt_lo = S("t_yt"), S("t_yt_hi"), S("t_yt_lo")
    t_up, t_silu, t_inter = S("t_up"), S("t_silu"), S("t_inter")
    t_it, t_it_hi, t_it_lo = S("t_it"), S("t_it_hi"), S("t_it_lo")
    t_down, t_scaled = S("t_down"), S("t_scaled")

    LAST = BATCHES

    def steady(engine, body):
        body(0, 0, 0)
        with engine.Fori(0, 2) as q:
            body(q * 3 + 1, 1, q)
            body(q * 3 + 2, 2, q)
            body(q * 3 + 3, 0, q + 1)
        body(LAST - 1, (LAST - 1) % SLOTS, (LAST - 1) // SLOTS)
        body(LAST, LAST % SLOTS, LAST // SLOTS)

    def known(b):
        return isinstance(b, int)

    def first(i):
        return known(i) and i == 0

    def shift(s, r, d):
        return (s + d) % SLOTS, r + (s + d) // SLOTS

    def uses16(r):
        return r * 16 + 16

    def pair(s, r, d, n):
        s, r = shift(s, r, d)
        return r * 2 + (2 * s + n) // PAIRS, (2 * s + n) % PAIRS

    T0, T1 = 8, TILES - 1
    assert (T1 - T0) % 2 == 0

    def steps(engine, body, before_loop=range(-4, T0), after_loop=range(T1, TILES + 4)):
        for t in before_loop:
            body(t, t % 2, lambda i: 0 <= i < TILES)
        with engine.Fori(T0 // 2, (T1 + 1) // 2) as q:
            body(q * 2, 0, lambda i: True)
            body(q * 2 + 1, 1, lambda i: True)
        for t in after_loop:
            body(t, t % 2, lambda i: 0 <= i < TILES)

    def late_pair(t):
        u = 2 * LAST + 1 + t if known(t) else None
        return u if known(t) and 2 * LAST <= u < PAIRS * EXPERTS else None

    def ok(i, live):
        return live(i) if known(i) else True

    def uses(t, d, par):
        return (t - par) * 8 + 16 * ((par + d) // 2 + 1)

    def one(w, e, i, n=1):
        w, i = (w[0], i) if i < KD else (w[1], i - KD)
        if not known(e):
            return w[:, bass.ds(e, 1), i:i + n].rearrange("p e i n -> p (e i n)")
        return w[:, e, i:i + n].rearrange("p i n -> p (i n)")

    ENTRIES_OUT = [16 + 16 * 2 * TOP * len(range(i, BATCHES, SLOTS)) for i in range(SLOTS)]

    OUT_FIRST = 8
    OUT_PARTS = OUT_FIRST // 2 + (LAST - 2) + 1

    block = nc.Block()
    with block:

        @block.sync
        def _(sp):
            def load_x(b, slot):
                src = xT[b] if known(b) else xT[bass.ds(b, 1)].rearrange("b p k n -> (b p) k n")
                sp.dma_start(x_raw[:, slot], src).then_inc(x_in[slot], 16)

            def adapter_of(b):
                i = slice(b, b + 1) if known(b) else bass.ds(b, 1)
                return sp.value_load(adapter_b[0:1, i], min_val=0, max_val=ADAPTERS - 1)

            def load_a(a):
                sp.dma_start(a_raw[:], aT[bass.ds(a, 1)].rearrange("a p k g r -> (a p) k g r")).then_inc(a_in, 16)

            def load_b(a):
                sp.dma_start(b_raw[:], bT[bass.ds(a, 1)].rearrange("a p n -> (a p) n")).then_inc(b_in, 16)

            def load_pair(e, i, sem):
                src = experts[i][e] if known(e) else experts[i][bass.ds(e, 1)].rearrange("e p n -> (e p) n")
                sp.dma_start(one(w_raw, e, 2 * i, 2), src).then_inc(sem, 16)

            def store_y(b, j):
                r = b * SEQ + j * P
                dst = y_rows[r:r + P, :] if known(b) else y_rows[bass.ds(sp.snap(r), P), :]
                sp.wait_ge(y_copied, b * 2 + j + 3)
                sp.dma_start(dst, y_sb[:, j]).then_inc(y_stored[j], 16)

            def start_out(tile, n):
                rows = slice(tile * P, (tile + n) * P) if known(tile) else bass.ds(sp.snap(tile * P), n * P)
                sp.dma_start(out[rows, :], x[rows, :]).then_inc(out_is_x, 16)

            load_x(0, 0)
            for k in range(KD):
                sp.dma_start(wt_raw[:, k], wT[:, k]).then_inc(wt_in[k], 16)
            sp.dma_start(w_nat[:], w).then_inc(w_nat_in, 16)
            sp.wait_ge(idx_in, 16)
            a = adapter_of(0)
            load_a(a)
            load_b(a)
            load_x(1, 1)
            for j in range(2):
                sp.dma_start(y_rows[TOKENS + j * P // 2:TOKENS + (j + 1) * P // 2], zeros[0:P // 2]).then_inc(y_stored[j], 16)

            def iteration(i, s, r):
                more = not (known(i) and i >= LAST - 1)
                if more and not first(i):
                    sp.wait_ge(y_done, i * 2)
                    load_x(i + 1, (s + 1) % SLOTS)
                if not (known(i) and i in (0, LAST)):
                    a_now = adapter_of(i)
                if more:
                    a = adapter_of(i + 1)
                    sp.wait_ge(a_lo_done, i + 1)
                    load_a(a)
                if not (known(i) and i in (0, LAST)):
                    sp.wait_ge(b_lo_done, i)
                    load_b(a_now)
                for n in range(2):
                    load_pair(*pair(s, r, 0, n), pairs_in[s][n])
                if not known(i):
                    start_out(i + OUT_FIRST - 1, 1)
                elif i == 0:
                    for tile in range(0, OUT_FIRST, 2):
                        start_out(tile, 2)
                elif i == LAST - 1:
                    start_out(OUT_FIRST + LAST - 2, BLOCKS - OUT_FIRST - (LAST - 2))
                if not first(i):
                    store_y(i - 1, 0)
                    store_y(i - 1, 1)

            steady(sp, iteration)
            def list_rows(i):
                i = slice(i, i + 1) if known(i) else bass.ds(i, 1)
                return slots[bass.ds(sp.value_load(block_i[0:1, i], min_val=0, max_val=ALL_BLOCKS - 1) * P, P), :]

            def load_list(rows, ring, sem, slot):
                sp.dma_start(ring[:, slot], rows).then_inc(sem[slot], 16)

            sp.wait_ge(tables_done, 1)
            first_rows = [list_rows(i) for i in range(2)]
            for i in range(SLOTS):
                sp.wait_ge(entry_out[i], ENTRIES_OUT[i])
            for i in range(FIRST_LISTS):
                load_list(first_rows[i] if i < 2 else list_rows(i), g_list, g_list_in, i)

            def step(t, par, live):
                if ok(t + 4, live):
                    rows = list_rows(t + 4)
                    sp.wait_ge(yg_in[par], uses(t, 0 if known(t) and t < 2 else 2, par))
                    load_list(rows, g_list, g_list_in, par)
                if ok(t - 1, live):
                    rows = list_rows(t - 1)
                    if not (known(t) and t - 3 < 0):
                        sp.wait_ge(added, (t - 2) * 16)
                    load_list(rows, s_list, s_list_in, (par + 1) % 2)

            sp.wait_ge(y_done, 2 * BATCHES + 2)
            for t in range(T0):
                step(t, t % 2, lambda i: 0 <= i < TILES)
                if t < len(late_in):
                    u = LATE * PAIRS + t
                    load_pair(u // PAIRS, u % PAIRS, late_in[t])
            with sp.Fori(T0 // 2, (TILES - 5) // 2) as q:
                step(q * 2, 0, lambda i: True)
                step(q * 2 + 1, 1, lambda i: True)
            for t in range((TILES - 5) // 2 * 2, TILES + 4):
                step(t, t % 2, lambda i: 0 <= i < TILES)
            sp.wait_ge(added, 16 * TILES)

        @block.scalar
        def _(act):
            act.dma_start(wg[:], w_gate).then_inc(wg_in, 16)
            act.dma_start(adapter_b[:], adapter.partition_broadcast(P)).then_inc(idx_in, 16)
            act.dma_start(smallc[:], consts[:, C_EXPERT:C_ALL]).then_inc(const_in, 16)

            def split_x(b, slot, r):
                act.wait_ge(x_in[slot], uses16(r))
                nc.scalar.copy(x_hi[:, slot], x_raw[:, slot]).then_inc(x_hi_done, 1)

            def split_a(b):
                act.wait_ge(a_in, (b + 1) * 16)
                if not first(b):
                    act.wait_ge(xa_done, b)
                for t in (a_hl, a_h0):
                    final = nc.scalar.copy(t[:, :, 0:AROWS].rearrange("p k (g c r) -> p k g c r", g=GROUPS, c=2)[:, :, :, 0, :], a_raw[:])
                final.then_inc(a_hi_done, 1)

            def split_b(b):
                act.wait_ge(b_in, (b + 1) * 16)
                if not first(b):
                    act.wait_ge(y_done, b * 2 + 2)
                nc.scalar.copy(b_st[:], b_raw[:]).then_inc(b_hi_done, 1)

            def split_pair(e, i):
                nc.scalar.copy(one(w_hi, e, 2 * i, 2), one(w_raw, e, 2 * i, 2)).then_inc(w_hi_done, 1)

            def copy_y(b, j):
                act.wait_ge(y_done, b * 2 + j + 3)
                act.wait_ge(y_stored[j], b * 16 + 16)
                nc.scalar.copy(y_sb[:, j], ps_y[j][:]).then_inc(y_copied, 1)

            def exp_gap(b):
                act.wait_ge(gap_done, b + 1)
                nc.scalar.activation(gap_exp[:], gap[:], ACT.Exp).then_inc(gap_exp_done, 1)

            split_x(0, 0, 0)
            for k in range(KD):
                act.wait_ge(wt_in[k], 16)
                nc.scalar.copy(wt_hi[:, k], wt_raw[:, k]).then_inc(wt_hi_done, 1)
            act.wait_ge(setup_done, 1)
            split_a(0)
            split_x(1, 1, 0)
            act.wait_ge(w_gate_done, 1)
            for t in (a_hl, a_h0):
                final = nc.scalar.copy(t[:, :, AROWS:AROWS + EXPERTS], ps_wg.rearrange("p (k e) -> p k e", k=KD))
            final.then_inc(w_gate_hi, 1)
            act.wait_ge(scal_done, 1)

            def iteration(i, s, r):
                if not first(i):
                    for n in range(2):
                        e, p = pair(s, r, -1, n)
                        slot, rr = shift(s, r, -1)
                        act.wait_ge(pairs_in[slot][n], uses16(rr))
                        split_pair(e, p)
                if not (known(i) and i == LAST):
                    act.wait_ge(xa_done, i + 1)
                    if not first(i):
                        act.wait_ge(logits_done, i)
                        act.wait_ge(xa_lo_done, i)
                    sc = scal[:, i:i + 1] if known(i) else scal[:, bass.ds(i, 1)]
                    nc.scalar.activation(xl[:], ps_xa[s], ACT.Copy, scale=sc).then_inc(xl_done, 1)
                    sc = scal[0:AROWS, i:i + 1] if known(i) else scal[0:AROWS, bass.ds(i, 1)]
                    nc.scalar.activation(xa_st[:, s], ps_xa[s][0:AROWS], ACT.Copy, scale=sc).then_inc(xa_hi_done, 1)
                if not first(i):
                    copy_y(i - 1, 0)
                if not (known(i) and i >= LAST - 1):
                    if not first(i):
                        split_x(i + 1, *shift(s, r, 1))
                    split_a(i + 1)
                if known(i) and i == LAST - 1:
                    exp_gap(i)
                if not first(i):
                    copy_y(i - 1, 1)
                if not (known(i) and i == LAST):
                    split_b(i)
                if not (known(i) and i >= LAST - 1):
                    exp_gap(i)

            steady(act, iteration)
            act.wait_ge(const_in, 16)
            nc.scalar.activation(silu_in[:], smallc[:, 0:1], ACT.Silu)

            def step(t, par, live):
                if ok(t - 1, live):
                    act.wait_ge(t_up, t)
                    if not (known(t) and t - 1 < 1):
                        act.wait_ge(t_it, t - 1)
                    nc.scalar.activation(inter[:], ps_h[(par + 1) % 2][:, 0:M], ACT.Silu).then_inc(t_silu, 1)
                if ok(t + 1, live):
                    act.wait_ge(t_yt, t + 2)
                    if not (known(t) and t < 1):
                        act.wait_ge(t_up, t)
                    nc.scalar.copy(yt_hi[:, (par + 1) % 2], ps_yt[:].rearrange("p (k n) -> p k n", k=KD)).then_inc(t_yt_hi, 1)
                if ok(t - 2, live):
                    act.wait_ge(t_down, t - 1)
                    act.wait_ge(s_list_in[par], uses(t, -2, par))
                    if not (known(t) and t - 2 < 2):
                        act.wait_ge(added, (t - 3) * 16)
                    nc.scalar.activation(scaled[:, par], ps_o[par][:], ACT.Copy,
                                         scale=s_list[:, par, 1:2].bitcast(F32)).then_inc(t_scaled, 1)
                if ok(t - 1, live):
                    act.wait_ge(t_it, t)
                    if not (known(t) and t - 1 < 2):
                        act.wait_ge(t_down, t - 2)
                    nc.scalar.copy(it_hi[:, (par + 1) % 2], ps_it[:, 0:M].rearrange("p (k n) -> p k n", k=KM)).then_inc(t_it_hi, 1)
                u = late_pair(t)
                if u is not None:
                    if u < LATE * PAIRS:
                        act.wait_ge(pairs_in[LAST % SLOTS][u % 2], uses16(LAST // SLOTS))
                    else:
                        act.wait_ge(late_in[u - LATE * PAIRS], 16)
                    split_pair(u // PAIRS, u % PAIRS)

            steps(act, step)

        @block.vector
        def _(dve):
            chained = [0]

            def chain(ins):
                chained[0] += 1
                ins.then_inc(dve_chain, 1)
                dve.wait_ge(dve_chain, chained[0])

            V = nc.vector
            V.memset(a_h0[:].bitcast(F32), 0.0)
            V.memset(ones[:], 1.0).then_inc(setup_done, 1)
            V.memset(before[:], 0.0).then_inc(y_copied, 1)
            V.memset(one8[:], 1.0).then_inc(y_copied, 1)
            V.memset(scal[AROWS:ROWS], 1.0).then_inc(y_done, 1)
            V.memset(entry[:, 0, :, 0], 0).then_inc(y_done, 1)

            def low(out, raw, high):
                return V.tensor_tensor(out, raw, high.bitcast(F32), ALU.subtract)

            def split_x(b, slot):
                dve.wait_ge(x_hi_done, b + 1)
                low(x_lo[:, slot], x_raw[:, slot], x_hi[:, slot]).then_inc(x_lo_done, 1)

            def split_a(b):
                dve.wait_ge(a_hi_done, b + 1)
                cols = a_hl[:, :, 0:AROWS].rearrange("p k (g c r) -> p k g c r", g=GROUPS, c=2)
                low(cols[:, :, :, 1, :], a_raw[:], cols[:, :, :, 0, :]).then_inc(a_lo_done, 1)

            split_x(0, 0)
            for k in range(KD):
                dve.wait_ge(wt_hi_done, k + 1)
                low(wt_lo[:, k], wt_raw[:, k], wt_hi[:, k]).then_inc(wt_lo_done, 1)
            dve.wait_ge(idx_in, 16)
            dve.wait_ge(const_in, 16)
            chain(V.tensor_copy(adapter_f[:], adapter_b[:]))
            chain(V.tensor_tensor(mask[:], adapter_f[:], const(C_ADAPTER, 1).to_broadcast([P, BATCHES]), ALU.is_equal))
            shape = [P, BATCHES, 2 * RANK]
            V.tensor_tensor(select[:], mask[:].unsqueeze(2).to_broadcast(shape),
                            const(C_SAME, 2 * RANK).unsqueeze(1).to_broadcast(shape), ALU.mult)
            chain(V.tensor_copy(gate[:], const(C_GATE, EXPERTS, ROWS).unsqueeze(1).to_broadcast([ROWS, BATCHES, EXPERTS])))
            shape = [AROWS, BATCHES, ADAPTERS]
            chain(V.tensor_tensor(scal_oh[:], adapter_f[0:AROWS].unsqueeze(2).to_broadcast(shape),
                                  expert_no[0:AROWS].unsqueeze(1).to_broadcast(shape), ALU.is_equal))
            dve.wait_ge(scal_in, 16)
            chain(V.tensor_tensor(scal_oh[:], scal_oh[:], scal_b[:].unsqueeze(1).to_broadcast(shape), ALU.mult))
            V.tensor_reduce(scal[0:AROWS], scal_oh[:], AX.X, ALU.add).then_inc(scal_done, 1)
            dve.wait_ge(gate_product, 1)
            V.tensor_copy(g_all[:], ps_g).then_inc(gate_copied, 1)
            split_a(0)
            split_x(1, 1)
            dve.wait_ge(w_gate_hi, 1)
            low(a_hl[:, :, AROWS + EXPERTS:ROWS], ps_wg.rearrange("p (k e) -> p k e", k=KD), a_hl[:, :, AROWS:AROWS + EXPERTS]).then_inc(w_gate_lo, 1)
            dve.wait_ge(gate_product, 2)
            V.tensor_copy(gate[0:2 * RANK].rearrange("p b e -> p (b e)"), ps_gate).then_inc(gate_copied, 1)
            dve.wait_ge(upper_in, 16)
            V.tensor_copy(upper[:], upper_raw[:]).then_inc(setup_done, 1)

            ROUTE, CHOICE = 12, 6
            THIRD = 2 * RANK

            class link:
                def __init__(self, b, n):
                    self.b, self.n = b, n

                def __call__(self, ins):
                    self.n += 1
                    ins.then_inc(dve_chain, 1)
                    dve.wait_ge(dve_chain, self.b * ROUTE + (SETUP + self.n))

            SETUP = chained[0]

            def choose(b, slot, ln):
                dve.wait_ge(logits_done, b + 1)
                V.tensor_scalar(token_no, token_no, float(SEQ), None, ALU.add)
                V.max(best[:, 0], ps_log[:, 0])
                ln(V.max(best[:, 1], ps_log[:, 1]))
                V.tensor_tensor(gap[:], best[:, :, 1], best[:, :, 0], ALU.subtract).then_inc(gap_done, 1)
                V.max_index(best_at[:, 0], best[:, 0], ps_log[:, 0])
                ln(V.max_index(best_at[:, 1], best[:, 1], ps_log[:, 1]))
                ln(V.tensor_copy(best_f[:], best_at[:, :, 0:TOP]))
                shape = [P, 2 * TOP, EXPERTS]
                ln(V.tensor_tensor(onehot[:].rearrange("p j k e -> p (j k) e"),
                                   best_f[:].rearrange("p j k -> p (j k)").unsqueeze(2).to_broadcast(shape),
                                   expert_no.unsqueeze(1).to_broadcast(shape), ALU.is_equal))
                ln(V.tensor_tensor(chosen[:], onehot[:, :, 0], onehot[:, :, 1], ALU.add))
                ln(V.tensor_tensor(between[:], before[:, slot], chosen[:, 0], ALU.add))
                V.tensor_tensor(before[:, (slot + 1) % SLOTS], between[:], chosen[:, 1], ALU.add).then_inc(chosen_done, 1)

            def weigh(b, slot, r, ln):
                dve.wait_ge(gap_exp_done, b + 1)
                dve.wait_ge(entry_out[slot], r * 16 * 2 * TOP + 16)
                e = entry[:, slot].bitcast(F32).rearrange("p (j k) c -> p j k c", j=2)
                ln(V.tensor_scalar(gap_den[:], gap_exp[:], 1.0, None, ALU.add))
                ln(V.reciprocal(e[:, :, 0, 1], gap_den[:]))
                V.tensor_tensor(e[:, :, 1, 1], gap_exp[:], e[:, :, 0, 1], ALU.mult)
                ln(V.tensor_copy(entry[:, slot, :, 0], token_no))

            def place(b, slot, ln):
                dve.wait_ge(rank_done, b + 1)
                ln(V.tensor_tensor(row_of[:], ps_rank, base_row.unsqueeze(1).to_broadcast([P, 2, EXPERTS]), ALU.add))
                for k in range(TOP):
                    final = V.tensor_tensor(row_oh[:, :, k], onehot[:, :, k], row_of[:], ALU.mult)
                ln(final)
                ln(V.tensor_reduce(row_f[:], row_oh[:].rearrange("p j k e -> p (j k) e"), AX.X, ALU.add))
                assert ln.n == ROUTE
                V.tensor_copy(row_no[:, slot], row_f[:]).then_inc(entry_done, 1)

            def split_odd(e, i, done):
                dve.wait_ge(w_hi_done, done)
                low(one(w_lo, e, 2 * i + 1), one(w_raw, e, 2 * i + 1), one(w_hi, e, 2 * i + 1)).then_inc(w_lo_dve, 1)

            def split_b(b):
                dve.wait_ge(b_hi_done, b + 1)
                rows = slice(2 * THIRD, AROWS)
                low(b_st[rows], b_raw[rows], b_st[rows]).then_inc(b_lo_done, 1)

            def iteration(i, s, r):
                if known(i) and i == LAST:
                    finish(i, s, r)
                    split_b(i - 1)
                    for u in range(2 * i - 4, 2 * i - 2):
                        split_odd(u // PAIRS, u % PAIRS, u + 1)
                    return
                nearly = known(i) and i == LAST - 1
                if nearly:
                    split_b(i - 1)
                    finish(i, s, r)
                    choose(i, s, link(i, 0))
                if not first(i) and not nearly:
                    split_b(i - 1)
                    for n in range(2):
                        split_odd(*pair(s, r, -1, n), i * 2 + (n - 1))
                    finish(i, s, r)
                dve.wait_ge(xa_hi_done, i + 1)
                rows = slice(THIRD, 2 * THIRD)
                low(xa_st[rows, s], xl[rows], xa_st[rows, s]).then_inc(xa_lo_done, 1)
                if not first(i) and not nearly:
                    choose(i, s, link(i, 0))
                if not nearly:
                    if not first(i):
                        split_x(i + 1, (s + 1) % SLOTS)
                    split_a(i + 1)
                if first(i):
                    choose(i, s, link(i, 0))

            def finish(i, s, r):
                ln = link(i - 1, CHOICE)
                weigh(i - 1, *shift(s, r, -1), ln)
                place(i - 1, (s - 1) % SLOTS, ln)

            steady(dve, iteration)
            chained[0] = SETUP + ROUTE * BATCHES
            dve.wait_ge(count_done, 1)
            shape = [1, EXPERTS, BLOCKS]
            chain(V.tensor_tensor(cmp_n[:], ps_count[0:1].unsqueeze(2).to_broadcast(shape),
                                  thresholds.unsqueeze(1).to_broadcast(shape), ALU.is_gt))
            chain(V.tensor_reduce(n_tiles[:], cmp_n[:], AX.X, ALU.add))
            chain(V.tensor_tensor_scan(tile_end[:], one8[:], n_tiles[:], 0.0, ALU.mult, ALU.add))
            chain(V.tensor_tensor(tile_rel[:], tile_no, tile_end[:, EXPERTS - 1:EXPERTS].to_broadcast([1, TILES]), ALU.add))
            shape = [1, TILES, EXPERTS - 1]
            chain(V.tensor_tensor(cmp_t[:], tile_rel[:].unsqueeze(2).to_broadcast(shape),
                                  tile_end[:, 0:EXPERTS - 1].unsqueeze(1).to_broadcast(shape), ALU.is_ge))
            V.tensor_tensor(cmp_s[:], cmp_t[:], n_tiles[:, 0:EXPERTS - 1].unsqueeze(1).to_broadcast(shape), ALU.mult)
            chain(V.tensor_reduce(expert_f[:], cmp_t[:], AX.X, ALU.add))
            chain(V.tensor_reduce(start_f[:], cmp_s[:], AX.X, ALU.add))
            V.tensor_copy(expert_i[:], expert_f[:])
            chain(V.scalar_tensor_tensor(block_f[:], expert_f[:], float(BLOCKS), tile_rel[:], ALU.mult, ALU.add))
            chain(V.tensor_tensor(block_f[:], block_f[:], start_f[:], ALU.subtract))
            V.tensor_scalar(block_i[:], block_f[:], float(SPARE), None, ALU.add).then_inc(tables_done, 1)
            for u in range(2 * LAST - 2, 2 * LAST):
                split_odd(u // PAIRS, u % PAIRS, u + 1)

            def step(t, par, live):
                if ok(t - 1, live):
                    dve.wait_ge(t_silu, t)
                    V.tensor_tensor(inter[:], inter[:], ps_h[(par + 1) % 2][:, M:2 * M], ALU.mult).then_inc(t_inter, 1)
                if ok(t + 1, live):
                    dve.wait_ge(t_yt_hi, t + 2)
                    s = (par + 1) % 2
                    low(yt_lo[:, s], ps_yt[:].rearrange("p (k n) -> p k n", k=KD), yt_hi[:, s]).then_inc(t_yt_lo, 1)
                if ok(t - 1, live):
                    dve.wait_ge(t_it_hi, t)
                    s = (par + 1) % 2
                    low(it_lo[:, s], ps_it[:, 0:M].rearrange("p (k n) -> p k n", k=KM), it_hi[:, s]).then_inc(t_it_lo, 1)
                u = late_pair(t)
                if u is not None:
                    dve.wait_ge(w_hi_done, u + 1)
                    e, i = u // PAIRS, u % PAIRS * 2
                    low(one(w_lo, e, i, 2), one(w_raw, e, i, 2), one(w_hi, e, i, 2)).then_inc(w_lo_dve, 1)

            steps(dve, step)

        @block.gpsimd
        def _(pool):
            pool.dma_start(b_nat[:], b_all).then_inc(b_nat_in, 16)
            pool.dma_start(scal_b[:], scalings.partition_broadcast(AROWS)).then_inc(scal_in, 16)
            pool.dma_start(upper_raw[:], consts[:, C_UPPER:C_UPPER + P]).then_inc(upper_in, 16)
            cuts = [ALL_BLOCKS * i // SLOTS * P for i in range(SLOTS + 1)]
            for i in range(SLOTS):
                pool.dma_start(slots[cuts[i]:cuts[i + 1]], empty_list[cuts[i]:cuts[i + 1]]).then_inc(entry_out[i], 16)
            pool.dma_start(out[TOKENS:TOKENS + P], zeros).then_inc(out_pad, 16)
            pool.dma_start(ident[:], consts[:, C_IDENT:C_IDENT + P]).then_inc(ident_in, 16)

            def carry_wait():
                pool.sem_inc(wait_carried, 1)

            for i in range(SLOTS):
                pool.wait_ge(entry_out[i], 16)

            def split_even(e, i, done):
                pool.wait_ge(w_hi_done, done)
                nc.gpsimd.tensor_tensor(one(w_lo, e, 2 * i), one(w_raw, e, 2 * i), one(w_hi, e, 2 * i).bitcast(F32),
                                        ALU.subtract).then_inc(w_lo_pool, 1)

            def list_entries(b, slot):
                pool.wait_ge(entry_done, b + 1)
                carry_wait()
                for i in range(2 * TOP):
                    pool.indirect_dma_start(slots, bass.IndirectOffsetOnAxis(row_no[:, slot, i:i + 1], 0), entry[:, slot, i], None).then_inc(entry_out[slot], 16)

            def iteration(i, s, r):
                for n in range(2):
                    split_even(*pair(s, r, -1, n), i * 2 + (n - 1))
                list_entries(i - 1, (s - 1) % SLOTS)

            with pool.Fori(0, 2) as q:
                iteration(q * 3 + 1, 1, q)
                iteration(q * 3 + 2, 2, q)
                iteration(q * 3 + 3, 0, q + 1)
            for b in (BATCHES - 2, BATCHES - 1):
                list_entries(b, b % SLOTS)
            for u in range(2 * LAST - 4, 2 * LAST):
                split_even(u // PAIRS, u % PAIRS, u + 1)
            for j in range(2):
                pool.wait_ge(y_stored[j], 16 * BATCHES + 16)
            pool.wait_ge(out_pad, 16)

            def step(t, par, live):
                if ok(t + 2, live):
                    slot = t + 2 if known(t) and t + 2 < FIRST_LISTS else par
                    pool.wait_ge(g_list_in[slot], 16 if slot != par or known(t) and t < 0 else uses(t, 2, par) - 16)
                    if not (known(t) and t < 0):
                        pool.wait_ge(t_yt, t + 1)
                    carry_wait()
                    pool.indirect_dma_start(yg[:, par], None, y_rows, bass.IndirectOffsetOnAxis(g_list[:, slot, 0:1], 0)).then_inc(yg_in[par], 16)
                if ok(t - 3, live):
                    s = (par + 1) % 2
                    pool.wait_ge(t_scaled, t - 2)
                    if known(t) and t == 3:
                        pool.wait_ge(out_is_x, 16 * OUT_PARTS)
                    if not (known(t) and t - 3 < 1):
                        pool.wait_ge(added, (t - 3) * 16)
                    carry_wait()
                    pool.indirect_dma_start(out, bass.IndirectOffsetOnAxis(s_list[:, s, 0:1], 0), scaled[:, s], None,
                                            compute_op=ALU.add).then_inc(added, 16)

            for t in range(-4, T0):
                step(t, t % 2, lambda i: 0 <= i < TILES)
            with pool.Fori(T0 // 2, (TILES - 3) // 2) as q:
                step(q * 2, 0, lambda i: True)
                step(q * 2 + 1, 1, lambda i: True)
            for t in range((TILES - 3) // 2 * 2, TILES + 4):
                step(t, t % 2, lambda i: 0 <= i < TILES)

        @block.tensor
        def _(pe):
            mm = nc.tensor.matmul

            def first_product(b, slot):
                pe.wait_ge(x_lo_done, b + 1)
                pe.wait_ge(a_lo_done, b + 1)
                for k in range(KD):
                    mm(ps_xa[slot], a_hl[:, k], x_hi[:, slot, k], start=(k == 0), stop=False)
                    final = mm(ps_xa[slot], a_h0[:, k], x_lo[:, slot, k], start=False, stop=(k == KD - 1))
                final.then_inc(xa_done, 1)

            def base(b, slot, j, chunks=range(KD), passes=(0, 1, 2)):
                if chunks[0] == 0 and passes[0] == 0:
                    pe.wait_ge(y_copied, b * 2 + j + 1)
                cols = slice(j * P, (j + 1) * P)
                for k in chunks:
                    for n in passes:
                        mm(ps_y[j][:], (x_lo if n == 2 else x_hi)[:, slot, k, cols], (wt_lo if n == 1 else wt_hi)[:, k],
                           start=(k == 0 and n == 0), stop=False)

            def delta(b, slot, j):
                if j == 0:
                    pe.wait_ge(xa_lo_done, b + 1)
                    pe.wait_ge(b_lo_done, b + 1)
                mm(ps_y[j][:], xa_st[:, slot, j * P:(j + 1) * P], b_st[:], start=False, stop=True).then_inc(y_done, 1)

            def logits(b):
                pe.wait_ge(xl_done, b + 1)
                if not first(b):
                    pe.wait_ge(chosen_done, b)
                g = gate[:, b] if known(b) else gate[:, bass.ds(b, 1)].rearrange("p b e -> p (b e)")
                for j in range(2):
                    final = mm(ps_log[:, j], xl[:, j * P:(j + 1) * P], g, start=True, stop=True)
                final.then_inc(logits_done, 1)

            def rank(b, slot):
                pe.wait_ge(chosen_done, b + 1)
                mm(ps_rank[:, 0], upper[:], chosen[:, 0], start=True, stop=False)
                mm(ps_rank[:, 0], ones[:], before[:, slot], start=False, stop=True)
                mm(ps_rank[:, 1], upper[:], chosen[:, 1], start=True, stop=False)
                mm(ps_rank[:, 1], ones[:], between[:], start=False, stop=True).then_inc(rank_done, 1)

            pe.wait_ge(wg_in, 16)
            pe.wait_ge(b_nat_in, 16)
            for k in range(KD):
                final = mm(ps_g, b_nat[:, k], wg[:, k], start=(k == 0), stop=(k == KD - 1))
            final.then_inc(gate_product, 1)
            pe.wait_ge(x_hi_done, 1)
            for k in range(KD):
                pe.wait_ge(wt_hi_done, k + 1)
                for j in range(2):
                    base(0, 0, j, (k,), (0,))
            pe.wait_ge(x_lo_done, 1)
            for k in range(KD):
                pe.wait_ge(wt_lo_done, k + 1)
                base(0, 0, 0, (k,), (1, 2))
            pe.wait_ge(w_nat_in, 16)
            for c in range(KD):
                for k in range(KD):
                    final = mm(ps_wg[:, c * EXPERTS:(c + 1) * EXPERTS], w_nat[:, k, c * P:(c + 1) * P], wg[:, k],
                               start=(k == 0), stop=(k == KD - 1))
            final.then_inc(w_gate_done, 1)
            pe.wait_ge(gate_copied, 1)
            for b in range(BATCHES):
                final = mm(ps_gate[:, b * EXPERTS:(b + 1) * EXPERTS], select[:, b], g_all[:], start=True, stop=True)
            final.then_inc(gate_product, 1)
            base(0, 0, 1, range(KD // 2), (1, 2))
            pe.wait_ge(w_gate_lo, 1)
            first_product(0, 0)
            base(0, 0, 1, range(KD // 2, KD), (1, 2))
            pe.wait_ge(gate_copied, 2)
            logits(0)
            first_product(1, 1)
            pe.wait_ge(setup_done, 2)
            rank(0, 0)
            delta(0, 0, 0)
            logits(1)
            delta(0, 0, 1)

            def iteration(i, s):
                before_it = (s - 1) % SLOTS
                base(i - 1, before_it, 0)
                rank(i - 1, before_it)
                first_product(i, s)
                base(i - 1, before_it, 1, range(KD // 2))
                delta(i - 1, before_it, 0)
                logits(i)
                base(i - 1, before_it, 1, range(KD // 2, KD))
                delta(i - 1, before_it, 1)

            with pe.Fori(0, 2) as q:
                iteration(q * 3 + 2, 2)
                iteration(q * 3 + 3, 0)
                iteration(q * 3 + 4, 1)
            b, slot = BATCHES - 1, (BATCHES - 1) % SLOTS
            base(b, slot, 0, range(1))
            rank(b, slot)
            mm(ps_count, ones[:], before[:, (slot + 1) % SLOTS], start=True, stop=True).then_inc(count_done, 1)
            base(b, slot, 0, range(1, KD))
            base(b, slot, 1, range(KD // 2))
            delta(b, slot, 0)
            base(b, slot, 1, range(KD // 2, KD))
            delta(b, slot, 1)

            def split(pairs):
                pe.wait_ge(w_lo_pool, min(pairs, 2 * LAST))
                pe.wait_ge(w_lo_dve, pairs)

            pe.wait_ge(w_lo_dve, 1)
            with pe.Fori(0, 8):
                for _ in range(4):
                    mm(bank[7][:], one(w_hi, 0, 0)[:, 0:P], one(w_hi, 0, 0), start=True, stop=True)
            split(PAIRS * (LATE - 1))
            pe.wait_ge(tables_done, 1)
            pe.wait_ge(ident_in, 16)

            def expert_of(i):
                i = slice(i, i + 1) if known(i) else bass.ds(i, 1)
                return pe.value_load(expert_i[0:1, i], min_val=0, max_val=EXPERTS - 1)

            def transpose(t, par, live):
                nxt = (par + 1) % 2
                if ok(t + 1, live):
                    pe.wait_ge(yg_in[nxt], uses(t, 1, par))
                    if not (known(t) and t + 1 < 1):
                        pe.wait_ge(t_yt_lo, t + 1)
                    for k in range(KD):
                        final = nc.tensor.transpose(ps_yt[:, k * P:(k + 1) * P], yg[:, nxt, k * P:(k + 1) * P], ident[:])
                    final.then_inc(t_yt, 1)

            def step(t, par, live):
                if ok(t, live):
                    e_up = expert_of(t)
                if ok(t - 2, live):
                    e_down = expert_of(t - 2)
                    pe.wait_ge(t_it_lo, t - 1)
                    if not (known(t) and t - 2 < 2):
                        pe.wait_ge(t_scaled, t - 3)
                    for k in range(KM):
                        hi = one(w_hi, e_down, KD + k)
                        lo = one(w_lo, e_down, KD + k)
                        mm(ps_o[par][:], it_hi[:, par, k], hi, start=(k == 0), stop=False)
                        mm(ps_o[par][:], it_lo[:, par, k], hi, start=False, stop=False)
                        final = mm(ps_o[par][:], it_hi[:, par, k], lo, start=False, stop=(k == KM - 1))
                    final.then_inc(t_down, 1)
                transpose(t, par, live)
                if ok(t - 1, live):
                    pe.wait_ge(t_inter, t)
                    if not (known(t) and t - 1 < 1):
                        pe.wait_ge(t_it_lo, t - 1)
                    for k in range(KM):
                        final = nc.tensor.transpose(ps_it[:, k * P:(k + 1) * P], inter[:, k * P:(k + 1) * P], ident[:])
                    final.then_inc(t_it, 1)
                if ok(t, live):
                    pe.wait_ge(t_yt_lo, t + 1)
                    if not (known(t) and t < 2):
                        pe.wait_ge(t_inter, t - 1)
                    for k in range(KD):
                        hi = one(w_hi, e_up, k)
                        lo = one(w_lo, e_up, k)
                        mm(ps_h[par][:], yt_hi[:, par, k], hi, start=(k == 0), stop=False)
                        mm(ps_h[par][:], yt_lo[:, par, k], hi, start=False, stop=False)
                        final = mm(ps_h[par][:], yt_hi[:, par, k], lo, start=False, stop=(k == KD - 1))
                    final.then_inc(t_up, 1)

            for t in range(-4, T0):
                if t in (LATE - 1, LATE):
                    split(PAIRS * (t + 1))
                step(t, t % 2, lambda i: 0 <= i < TILES)
            split(PAIRS * EXPERTS)
            steps(pe, step, before_loop=())


def kernel(**inputs):
    import concourse.bacc as bacc
    from concourse.bass_utils import run_bass_kernel_spmd as run

    n = {k: np.asarray(v) for k, v in inputs.items()}
    x = np.ascontiguousarray(n["x"].reshape(TOKENS, D))
    consts, empty_list, zeros = constants()
    wi = np.concatenate([n["L0_ffn_wi_0"], n["L0_ffn_wi_1"]], axis=2).reshape(EXPERTS, KD, P, 2 * M)
    wo = n["L0_ffn_wo"].reshape(EXPERTS, KM, P, D)
    a = n["L0_cond_A"].reshape(ADAPTERS, RANK, KD, 1, P).transpose(0, 4, 2, 3, 1)
    a = np.tile(a, (1, 1, 1, GROUPS, 1))
    b = np.tile(n["L0_cond_Bm"].transpose(0, 2, 1), (1, 2 * GROUPS, 1))
    arrays = {
        "xT": x.reshape(BATCHES, SEQ, KD, P).transpose(0, 3, 2, 1),
        "x": x,
        "wT": n["L0_cond_W"].T.reshape(KD, P, D).transpose(1, 0, 2),
        "w": n["L0_cond_W"].reshape(KD, P, D).transpose(1, 0, 2),
        "b_all": n["L0_cond_Bm"].transpose(1, 0, 2).reshape(KD, P, ADAPTERS * RANK).transpose(1, 0, 2),
        "aT": a,
        "bT": b,
        "scalings": n["L0_cond_scalings"],
        "adapter": n["itok_B_0_6"],
        "w_gate": n["L0_ffn_w_gate"].reshape(KD, P, EXPERTS).transpose(1, 0, 2),
        "experts": np.concatenate([wi, wo], axis=1).reshape(EXPERTS, PAIRS, 2, P, D).transpose(1, 0, 3, 2, 4).reshape(PAIRS, EXPERTS, P, 2 * D),
        "consts": consts,
        "empty_list": empty_list,
        "zeros": zeros,
    }
    nc = bacc.Bacc("TRN2", target_bir_lowering=False, num_devices=1, dynamic_dma_scratch_size=SCRATCH)
    given, aps = {}, {}
    for name, v in arrays.items():
        v = np.ascontiguousarray(v)
        given[f"in_{name}"] = v
        aps[name] = nc.dram_tensor(f"in_{name}", v.shape, mybir.dt.from_np(v.dtype), kind="ExternalInput").ap()
    out = nc.dram_tensor("out_0", (TOKENS + P, D), F32, kind="ExternalOutput").ap()
    build(nc, out=out, **aps)
    r = run(nc, [given], core_ids=[0])
    return r.results[0]["out_0"][:TOKENS].reshape(BATCHES, SEQ, D)
```
